# Optimizing a Trainium2 kernel written in Bass

```python
import numpy as np
import jax
import jax.numpy as jnp

def _softmax(x, axis=-1):
    return jax.nn.softmax(x, axis=axis)

def _gelu(x):
    return jax.nn.gelu(x, approximate=True)

def _silu(x):
    return jax.nn.silu(x)

def _sigmoid(x):
    return jax.nn.sigmoid(x)

def _layernorm(x, axis=-1, eps=1e-05):
    m = jnp.mean(x, axis=axis, keepdims=True)
    v = jnp.var(x, axis=axis, keepdims=True)
    return (x - m) / jnp.sqrt(v + eps)

def _scatter_add(tgt, idx, src, axis=0):
    return tgt.at[idx].add(src)

def _segment_sum(src, seg, n):
    return jax.ops.segment_sum(src, seg, n)
kernel_name = 'mk_cond_resid_d2_seqx_r2_08221c'

def setup_inputs(seed: int=0):
    np.random.seed(seed)
    _w = jnp.asarray

    def _rec_inputs():
        import jax
        import jax.numpy as jnp
        _rk = jax.random.key(seed)
        x = -0.0003929 + 0.9999 * jax.random.normal(jax.random.fold_in(_rk, 1), (4, 1024, 1024), jnp.float32)
        _lenS = 1024 - jax.random.randint(jax.random.fold_in(_rk, 7), (4,), 0, max(1, 1024 // 4) + 1, jnp.int32)
        _lenS2 = 1024 - jax.random.randint(jax.random.fold_in(_rk, 8), (4,), 0, max(1, 1024 // 4) + 1, jnp.int32)
        cond_2048 = 0.00782532 + 1.00527 * jax.random.normal(jax.random.fold_in(_rk, 11), (4, 1024), jnp.float32)
        return (x, cond_2048)
    x, cond_2048 = _rec_inputs()

    def _L0_cond_setup():
        import jax, jax.numpy as jnp
        import numpy as np
        HEADS = 16
        EPS = 1e-06

        def _rms_norm(x, g):
            xf = x.astype(jnp.float32)
            y = xf * jax.lax.rsqrt(jnp.mean(xf * xf, axis=-1, keepdims=True) + EPS)
            return y.astype(x.dtype) * g
        key = jax.random.key(seed)
        ks = jax.random.split(key, 6)
        b, n, dim, emb_dim = (4, 1024, 1024, 1024)
        d_head = dim // HEADS
        return {'x': jax.random.normal(ks[0], (b, n, dim), jnp.float32), 'emb': jax.random.normal(ks[1], (b, 1, emb_dim), jnp.float32), 'W_emb': jax.random.normal(ks[2], (emb_dim, 2 * dim), jnp.float32) * emb_dim ** (-0.5), 'b_emb': jnp.zeros((2 * dim,), jnp.float32), 'g_norm': jnp.ones((dim,), jnp.float32), 'W_qkv': jax.random.normal(ks[3], (dim, 3 * dim), jnp.float32) * dim ** (-0.5), 'g_q': jnp.ones((d_head,), jnp.float32), 'g_k': jnp.ones((d_head,), jnp.float32), 'W_out': jax.random.normal(ks[4], (dim, dim), jnp.float32) * dim ** (-0.5)}
    _L0_cond_all = _L0_cond_setup()
    _L0_cond_in = {k: v for k, v in _L0_cond_all.items() if k in ('W_emb', 'b_emb', 'g_norm', 'W_qkv', 'g_q', 'g_k', 'W_out')}
    del _L0_cond_all

    def _L1_cond_setup():
        import jax, jax.numpy as jnp
        import numpy as np
        key = jax.random.key(seed)
        k1, k2, k3 = jax.random.split(key, 3)
        B, L, D, K = (4, 2048, 1024, 4)
        x = jax.random.normal(k1, (B, L, D), dtype=jnp.float32)
        w = jax.random.normal(k2, (K, 1, D), dtype=jnp.float32) * 0.1
        b = jax.random.normal(k3, (D,), dtype=jnp.float32) * 0.1
        return {'x': x, 'w': w, 'b': b}
    _L1_cond_all = _L1_cond_setup()
    _L1_cond_in = {k: v for k, v in _L1_cond_all.items() if k in ('b',)}
    del _L1_cond_all
    return {'x': x, 'cond_2048': cond_2048, 'L0_cond_W_emb': _L0_cond_in['W_emb'], 'L0_cond_b_emb': _L0_cond_in['b_emb'], 'L0_cond_g_norm': _L0_cond_in['g_norm'], 'L0_cond_W_qkv': _L0_cond_in['W_qkv'], 'L0_cond_g_q': _L0_cond_in['g_q'], 'L0_cond_g_k': _L0_cond_in['g_k'], 'L0_cond_W_out': _L0_cond_in['W_out'], 'L1_cond_b': _L1_cond_in['b']}

def reference(x, cond_2048, L0_cond_W_emb, L0_cond_b_emb, L0_cond_g_norm, L0_cond_W_qkv, L0_cond_g_q, L0_cond_g_k, L0_cond_W_out, L1_cond_b):
    import jax
    import jax.numpy as jnp

    def _L0_cond_ref(x, emb, W_emb, b_emb, g_norm, W_qkv, g_q, g_k, W_out):
        import jax, jax.numpy as jnp
        import numpy as np
        HEADS = 16
        EPS = 1e-06

        def _rms_norm(x, g):
            xf = x.astype(jnp.float32)
            y = xf * jax.lax.rsqrt(jnp.mean(xf * xf, axis=-1, keepdims=True) + EPS)
            return y.astype(x.dtype) * g
        b, n, dim = x.shape
        h = HEADS
        d = dim // h
        scale_shift = emb @ W_emb + b_emb
        scale, shift = jnp.split(scale_shift, 2, axis=-1)
        xn = _rms_norm(x, g_norm) * (1.0 + scale) + shift
        qkv = xn @ W_qkv
        qkv = qkv.reshape(b, n, 3, h, d)
        q, k, v = jnp.moveaxis(qkv, 2, 0)
        q = jnp.swapaxes(q, 1, 2)
        k = jnp.swapaxes(k, 1, 2)
        v = jnp.swapaxes(v, 1, 2)
        q = _rms_norm(q, g_q)
        k = _rms_norm(k, g_k)
        logits = jnp.einsum('bhqd,bhkd->bhqk', q, k) * d ** (-0.5)
        attn = jax.nn.softmax(logits, axis=-1)
        o = jnp.einsum('bhqk,bhkd->bhqd', attn, v)
        o = jnp.swapaxes(o, 1, 2).reshape(b, n, dim)
        return o + o @ W_out

    def _L1_cond_ref(x, w, b):
        import jax, jax.numpy as jnp
        import numpy as np
        'Depthwise causal conv1d, channel-last.\n            x: (B, L, D); w: (K, 1, D); b: (D,). Returns (B, L, D).\n            Matches torch: Conv1d(D, D, K, groups=D, padding=K-1)(x.T)[..., :L].T\n            which is exactly a causal conv (left pad K-1, trim to L).\n            '
        K = w.shape[0]
        D = x.shape[-1]
        y = jax.lax.conv_general_dilated(x, w, window_strides=(1,), padding=[(K - 1, 0)], feature_group_count=D, dimension_numbers=('NWC', 'WIO', 'NWC'))
        return y + b
    x = x + _L0_cond_ref(x, cond_2048[:, None, :], L0_cond_W_emb, L0_cond_b_emb, L0_cond_g_norm, L0_cond_W_qkv, L0_cond_g_q, L0_cond_g_k, L0_cond_W_out)
    x = x + _L1_cond_ref(x, cond_2048[:, None, :], L1_cond_b)
    return x

_drawn_inputs = setup_inputs


def setup_inputs(seed=0):
    import zlib

    import numpy as np

    out = dict(_drawn_inputs(seed))
    spreads = {'L0_cond_b_emb': (0.0, 0.1),
     'L0_cond_g_norm': (1.0, 0.578),
     'L0_cond_g_q': (1.0, 0.6),
     'L0_cond_g_k': (1.0, 0.6)}
    factors = {}
    for name, (base, spread) in spreads.items():
        noise = np.random.default_rng([zlib.crc32(name.encode()), seed]).standard_normal(out[name].shape)
        drawn = base * np.exp(spread * noise) if base else spread * noise
        out[name] = jnp.asarray(drawn.astype(out[name].dtype))
    for name, factor in factors.items():
        out[name] = (out[name] * factor).astype(out[name].dtype)
    return out
```

```python
from contextlib import ExitStack

import numpy as np

import concourse.bass as bass
from concourse import mybir

P = 128
F32 = mybir.dt.float32
F16 = mybir.dt.float16
U32 = mybir.dt.uint32
I32 = mybir.dt.int32
ALU = mybir.AluOpType
ACT = mybir.ActivationFunctionType
AX = mybir.AxisListType
RMAX = bass.bass_isa.ReduceOp.max

EPS = 1e-6
DH = 64
LAG = 4
X_UP = 256.0
W_UP = 1024.0
QKV_DOWN = 2.0 ** -16
QK_UP = 64.0
P_SHIFT = 12 * float(np.log(2.0))
EXPONENT = 0x7F800000
TINY = 1e-30

PLAN = {
    8: dict(sq0=4, ss0=4, n0=5, hi0=5, lo0=6, th0=7, te0=7,
            sq1=8, ss1=8, n1=9, hi1=10, lo1=10, th1=11, te1=11,
            xs=1, xr=1, xh=2, xt=9, xe=9, xhi=9, xlo=9, xst=12,
            ld=6, s=7, ot=8, oe=8, ohi=8, olo=8, op0a=9, op0b=10, y0=11, op1a=11, op1b=12,
            y1=13, yt0=12, yt1=13, ye0=13, ye1=14, cv0=13, cv1=14, fin=15),
    4: dict(sq0=2, ss0=2, n0=2, hi0=3, lo0=3, th0=4, te0=4,
            sq1=4, ss1=4, n1=4, hi1=4, lo1=4, th1=6, te1=6,
            xs=1, xr=1, xh=1, xt=5, xe=5, xhi=5, xlo=5, xst=6,
            ld=5, s=5, ot=5, oe=5, ohi=5, olo=5, op0a=6, op0b=6, y0=6, op1a=7, op1b=7,
            y1=7, yt0=7, yt1=7, ye0=7, ye1=7, cv0=7, cv1=7, fin=7),
}


def need(eng, sem, count):
    if isinstance(count, int) and count <= 0:
        return
    eng.wait_ge(sem, count)


def dims(x, W_qkv):
    B, N, D = x.shape
    K = D // P
    assert N == D and K in PLAN and W_qkv.shape == (D, 3 * D)
    return B, N, D, K


def bass_cond_attention_conv(nc, x, cond, W_emb, b_emb, g_norm, W_qkv, g_q, g_k, W_out, b_conv, out):
    B, N, D, K = dims(x, W_qkv)
    U = B * K
    with ExitStack() as ctx:
        def sb(name, shape, dt):
            return ctx.enter_context(nc.sbuf_tensor(name, shape, dt))

        const = dict(
            eye32=sb("eye32", [P, P], F32), eye16=sb("eye16", [P, P], F16),
            wo=sb("wo", [P, K, 2, D], F16),
            mod_a=sb("mod_a", [P, U, K], F32),
            mod_s=sb("mod_s", [P, U, K], F32),
            eps_u=sb("eps_u", [P, U], F32),
            v_scale=sb("v_scale", [P, U], F32),
            y_scale=sb("y_scale", [P, U], F32),
            carry=sb("carry", [P, U], F32),
            o_row=sb("o_row", [P, K], F32),
            g_qk=sb("g_qk", [P, DH], F32),
            l_scale=sb("l_scale", [P, 1], F32),
            taps=sb("taps", [P, B, K], F32), conv_b=sb("conv_b", [P, K], F32),
            power=sb("power", [P, 4 * K], F32),
        )
        w_dram = nc.dram_tensor("w_dram", [K, P, K, 2, 6 * DH], F16, kind="Internal").ap()
        xn_dram = nc.dram_tensor("xn_dram", [U, P, K * 2 * P], F16, kind="Internal").ap()
        o_dram = nc.dram_tensor("o_dram", [U * P, D], F32, kind="Internal").ap()
        prepare(nc, const, w_dram, x, cond, W_emb, b_emb, g_norm, W_qkv, g_q, g_k, W_out, b_conv)
        main(nc, const, w_dram, xn_dram, o_dram, x, W_qkv, out)


def prepare(nc, const, w_dram, x, cond, W_emb, b_emb, g_norm, W_qkv, g_q, g_k, W_out, b_conv):
    B, N, D, K = dims(x, W_qkv)
    NE = 2 * D // 512
    rows = B * K + 4 * K
    row_embb, row_g, row_cb = B * K, B * K + 2 * K, B * K + 3 * K
    with ExitStack() as ctx:
        def sb(name, shape, dt):
            return ctx.enter_context(nc.sbuf_tensor(name, shape, dt))

        def psum(name, shape, dt):
            return ctx.enter_context(nc.psum_tensor(name, shape, dt))

        def sem(name):
            return ctx.enter_context(nc.semaphore(name))

        small = sb("small", [rows, P], F32)
        smallT = sb("smallT", [P, rows], F32)
        emb_w = sb("emb_w", [P, 2, 2 * D], F32)
        wq_raw = sb("wq_raw", [P, 3, 3 * D], F32)
        wq_pair = sb("wq_pair", [P, 2, K, 2, 6 * DH], F16)
        wo_raw = sb("wo_raw", [P, 2, D], F32)
        ss_row = sb("ss_row", [B, 2 * D], F32)
        ssT = sb("ssT", [P, 2 * K, B], F32)
        mod = sb("mod", [P, 2, K, B], F32)
        wide = sb("wide", [P, 2, K, B], F32)
        gq = sb("gq", [P, 2, DH], F32)
        wq_max = sb("wq_max", [P, K], F32)
        wq_two = sb("wq_two", [P, K], F32)
        wq_inv = sb("wq_inv", [P, K], F32)
        wo_max = sb("wo_max", [P, K], F32)
        wo_two = sb("wo_two", [P, K], F32)
        wo_inv = sb("wo_inv", [P, K], F32)
        top = sb("top", [P, B + 1], F32)
        topr = sb("topr", [P, B + 1], F32)
        two = sb("two", [P, B + 1], F32)
        twoi = sb("twoi", [P, B + 1], F32)
        gmax = sb("gmax", [P, 4], F32)
        tmpb = sb("tmpb", [P, 3, B], F32)
        ps_row = psum("ps_row", [B, 2 * D], F32)
        ps_t = psum("ps_t", [P, 512], F32)
        ps_s = psum("ps_s", [P, 512], F32)

        small_in = sem("small_in")
        g_in = sem("g_in")
        emb_in = [sem(f"emb_in{i}") for i in range(2)]
        wq_in = [sem(f"wq_in{i}") for i in range(3)]
        wo_in = [sem(f"wo_in{i}") for i in range(2)]
        wq_out = [sem(f"wq_out{i}") for i in range(2)]
        eye = sem("eye")
        eyed = sem("eyed")
        small_t = sem("small_t")
        small_c = sem("small_c")
        emb_mm = sem("emb_mm")
        emb_row = sem("emb_row")
        emb_t = sem("emb_t")
        dve = sem("dve_step")
        wq_scaled = sem("wq_scaled")
        wq_hi = sem("wq_hi")
        wq_lo = sem("wq_lo")
        wo_scaled = sem("wo_scaled")
        wo_hi = sem("wo_hi")
        wo_lo = sem("wo_lo")
        top_in = sem("top_in")
        top_all = sem("top_all")
        emb_v = W_emb.rearrange("(c p) n -> c p n", p=P)
        wq_v = W_qkv.rearrange("(c p) n -> c p n", p=P)
        wo_v = W_out.rearrange("(c p) n -> c p n", p=P)
        block = ctx.enter_context(nc.Block())

        def store_wq(sp, c):
            sp.wait_ge(wq_hi, 3 * (c + 1))
            sp.wait_ge(wq_lo, c + 1)
            sp.dma_start(w_dram[:, :, c].rearrange("h p s n -> p h (s n)"),
                         wq_pair[:, c % 2].rearrange("p h s n -> p h (s n)")).then_inc(wq_out[c % 2], 16)

        def by_head(c, s, j):
            return wq_pair[:, c % 2, :, s, :].rearrange("p g (h j d) -> p g h j d", h=2, j=3)[:, :, :, j, :]

        def raw_by_head(c, j):
            return wq_raw[:, c % 3, j * D:(j + 1) * D].rearrange("p (g h d) -> p g h d", h=2, d=DH)

        @block.sync
        def _(sp):
            sp.dma_start(small[0:B * K, :], cond.rearrange("b (c p) -> (b c) p", p=P)).then_inc(small_in, 16)
            sp.dma_start(small[row_embb:row_g, :], b_emb.rearrange("(c p) -> c p", p=P)).then_inc(small_in, 16)
            sp.dma_start(small[row_g:row_cb, :], g_norm.rearrange("(c p) -> c p", p=P)).then_inc(small_in, 16)
            sp.dma_start(small[row_cb:rows, :], b_conv.rearrange("(c p) -> c p", p=P)).then_inc(small_in, 16)
            sp.dma_start(gq[:, 0, :], g_q.rearrange("(a d) -> a d", a=1).to_broadcast([P, DH])).then_inc(g_in, 16)
            sp.dma_start(gq[:, 1, :], g_k.rearrange("(a d) -> a d", a=1).to_broadcast([P, DH])).then_inc(g_in, 16)
            for c in range(K):
                need(sp, wq_lo, c - 2)
                sp.dma_start(wq_raw[:, c % 3, :], wq_v[c]).then_inc(wq_in[c % 3], 16)
                need(sp, emb_mm, c - 1)
                sp.dma_start(emb_w[:, c % 2, :], emb_v[c]).then_inc(emb_in[c % 2], 16)
                if c:
                    store_wq(sp, c - 1)
            store_wq(sp, K - 1)
            for c in range(K):
                need(sp, wo_lo, c - 1)
                sp.dma_start(wo_raw[:, c % 2, :], wo_v[c]).then_inc(wo_in[c % 2], 16)
            sp.wait_ge(wq_out[0], 16 * (K // 2))
            sp.wait_ge(wq_out[1], 16 * (K // 2))

        @block.gpsimd
        def _(pool):
            nc.gpsimd.memset(const["eye32"][:], 0.0).then_inc(eye, 1)
            nc.gpsimd.memset(const["power"][:], -0.5)
            nc.gpsimd.memset(const["carry"][:], 1.0).then_inc(eye, 1)
            pool.wait_ge(eye, 2)
            nc.gpsimd.affine_select(out=const["eye32"][:], in_=const["eye32"][:], compare_op=ALU.not_equal,
                                    fill=1.0, base=0, pattern=[[-1, P]], channel_multiplier=1).then_inc(eye, 1)
            nc.gpsimd.memset(const["carry"][:].rearrange("p (b k) -> p b k", k=K)[:, :, 0:1], 0.0).then_inc(eye, 1)
            pool.wait_ge(eye, 4)
            nc.gpsimd.tensor_copy(const["eye16"][:], const["eye32"][:]).then_inc(eyed, 1)
            for c in range(K):
                pool.wait_ge(wq_hi, 3 * (c + 1))
                for j in range(3):
                    last = nc.gpsimd.tensor_tensor(by_head(c, 1, j), raw_by_head(c, j), by_head(c, 0, j),
                                                   ALU.subtract)
                last.then_inc(wq_lo, 1)
            for c in range(K):
                pool.wait_ge(wo_hi, c + 1)
                nc.gpsimd.tensor_tensor(const["wo"][:, c, 1, :], wo_raw[:, c % 2, :], const["wo"][:, c, 0, :],
                                        ALU.subtract).then_inc(wo_lo, 1)
            pool.wait_ge(top_in, 1)
            nc.gpsimd.partition_all_reduce(topr[:], top[:], P, RMAX).then_inc(top_all, 1)

        @block.scalar
        def _(act):
            for c in range(K):
                act.wait_ge(wq_scaled, c + 1)
                if c >= 2:
                    act.wait_ge(wq_out[c % 2], 16 * (c // 2))
                for j in range(3):
                    nc.scalar.activation(by_head(c, 0, j), raw_by_head(c, j), ACT.Copy).then_inc(wq_hi, 1)
            act.wait_ge(emb_mm, K)
            nc.scalar.activation(ss_row[:], ps_row[:], ACT.Copy).then_inc(emb_row, 1)
            for c in range(K):
                act.wait_ge(wo_scaled, c + 1)
                nc.scalar.activation(const["wo"][:, c, 0, :], wo_raw[:, c % 2, :], ACT.Copy).then_inc(wo_hi, 1)

        @block.tensor
        def _(pe):
            pe.wait_ge(small_in, 64)
            pe.wait_ge(eyed, 1)
            nc.tensor.transpose(ps_s[:, 0:rows], small[:], const["eye32"][0:rows, 0:rows]).then_inc(small_t, 1)
            pe.wait_ge(small_c, 1)
            cT = smallT[:, 0:B * K].rearrange("p (b c) -> p c b", c=K)
            for c in range(K):
                pe.wait_ge(emb_in[c % 2], 16 * (c // 2 + 1))
                for n in range(NE):
                    last = nc.tensor.matmul(ps_row[:, n * 512:(n + 1) * 512], cT[:, c, :],
                                            emb_w[:, c % 2, n * 512:(n + 1) * 512], start=(c == 0), stop=(c == K - 1))
                last.then_inc(emb_mm, 1)
            pe.wait_ge(emb_row, 1)
            for m in range(2 * K):
                last = nc.tensor.transpose(ps_t[:, m * B:(m + 1) * B], ss_row[:, m * P:(m + 1) * P],
                                           const["eye32"][0:B, 0:B])
            last.then_inc(emb_t, 1)

        @block.vector
        def _(v):
            steps = [0]

            def step(ins):
                steps[0] += 1
                ins.then_inc(dve, 1)
                v.wait_ge(dve, steps[0])

            def power_of_two(out, in_):
                step(nc.vector.tensor_scalar(in_, in_, TINY, None, ALU.max))
                step(nc.vector.tensor_scalar(out.bitcast(U32), in_.bitcast(U32), EXPONENT, None, ALU.bitwise_and))

            v.wait_ge(small_t, 1)
            nc.vector.tensor_copy(smallT[:], ps_s[:, 0:rows]).then_inc(small_c, 1)
            v.wait_ge(g_in, 32)
            step(nc.vector.tensor_tensor(const["g_qk"][:], gq[:, 0, :], gq[:, 1, :], ALU.mult))
            step(nc.vector.tensor_reduce(gmax[:, 0:1], const["g_qk"][:], axis=AX.X, op=ALU.max,
                                         apply_absolute_value=True))
            power_of_two(gmax[:, 1:2], gmax[:, 0:1])
            step(nc.vector.reciprocal(gmax[:, 2:3], gmax[:, 1:2]))
            step(nc.vector.tensor_scalar(const["g_qk"][:], const["g_qk"][:], gmax[:, 2:3], None, ALU.mult))
            step(nc.vector.tensor_scalar(const["l_scale"][:], gmax[:, 1:2], DH ** -0.5 / QK_UP ** 2, None, ALU.mult))
            for c in range(K):
                v.wait_ge(wq_in[c % 3], 16 * (c // 3 + 1))
                step(nc.vector.tensor_reduce(wq_max[:, c:c + 1], wq_raw[:, c % 3, :], axis=AX.X, op=ALU.max,
                                             apply_absolute_value=True))
                power_of_two(wq_two[:, c:c + 1], wq_max[:, c:c + 1])
                step(nc.vector.reciprocal(wq_inv[:, c:c + 1], wq_two[:, c:c + 1]))
                nc.vector.tensor_scalar(wq_raw[:, c % 3, :], wq_raw[:, c % 3, :], wq_inv[:, c:c + 1], W_UP,
                                        ALU.mult, ALU.mult).then_inc(wq_scaled, 1)
            for c in range(K):
                v.wait_ge(wo_in[c % 2], 16 * (c // 2 + 1))
                step(nc.vector.tensor_reduce(wo_max[:, c:c + 1], wo_raw[:, c % 2, :], axis=AX.X, op=ALU.max,
                                             apply_absolute_value=True))
                power_of_two(wo_two[:, c:c + 1], wo_max[:, c:c + 1])
                step(nc.vector.reciprocal(wo_inv[:, c:c + 1], wo_two[:, c:c + 1]))
                nc.vector.tensor_scalar(wo_raw[:, c % 2, :], wo_raw[:, c % 2, :], wo_inv[:, c:c + 1], W_UP,
                                        ALU.mult, ALU.mult).then_inc(wo_scaled, 1)
            v.wait_ge(emb_t, 1)
            step(nc.vector.tensor_tensor(
                ssT[:], ps_t[:, 0:2 * K * B].rearrange("p (m b) -> p m b", b=B),
                smallT[:, row_embb:row_g].rearrange("p (m a) -> p m a", a=1).to_broadcast([P, 2 * K, B]), ALU.add))
            step(nc.vector.tensor_scalar(mod[:, 0], ssT[:, 0:K, :], 1.0, None, ALU.add))
            step(nc.vector.tensor_tensor(
                mod[:, 0], mod[:, 0],
                smallT[:, row_g:row_cb].rearrange("p (m a) -> p m a", a=1).to_broadcast([P, K, B]), ALU.mult))
            step(nc.vector.tensor_copy(mod[:, 1], ssT[:, K:2 * K, :]))
            for i in range(2):
                step(nc.vector.tensor_tensor(
                    mod[:, i], mod[:, i], wq_two[:].rearrange("p (m a) -> p m a", a=1).to_broadcast([P, K, B]),
                    ALU.mult))
            for b in range(B):
                step(nc.vector.tensor_reduce(top[:, b:b + 1], mod[:, :, :, b], axis=AX.XY, op=ALU.max,
                                             apply_absolute_value=True))
            step(nc.vector.tensor_reduce(top[:, B:B + 1], wo_two[:], axis=AX.X, op=ALU.max))
            nc.vector.memset(gmax[:, 3:4], 0.0).then_inc(top_in, 1)
            v.wait_ge(top_all, 1)
            power_of_two(two[:], topr[:])
            step(nc.vector.reciprocal(twoi[:], two[:]))
            step(nc.vector.tensor_scalar(tmpb[:, 0], twoi[:, 0:B], X_UP, None, ALU.mult))
            for i, name in enumerate(("mod_a", "mod_s")):
                step(nc.vector.tensor_tensor(
                    wide[:, i], mod[:, i],
                    tmpb[:, 0].rearrange("p (a b) -> p a b", a=1).to_broadcast([P, K, B]), ALU.mult))
                for b in range(B):
                    step(nc.vector.tensor_copy(
                        const[name][:, b * K:(b + 1) * K, :],
                        wide[:, i, :, b].rearrange("p (a k) -> p a k", a=1).to_broadcast([P, K, K])))
            down = 1.0 / (X_UP * W_UP * QKV_DOWN)
            step(nc.vector.tensor_scalar(tmpb[:, 1], two[:, 0:B], down, None, ALU.mult))

            def by_unit(name):
                return const[name][:].rearrange("p (b k) -> p b k", k=K)

            def column(ap):
                return ap.rearrange("p (b a) -> p b a", a=1).to_broadcast([P, B, K])

            step(nc.vector.tensor_copy(by_unit("v_scale"), column(tmpb[:, 1])))
            step(nc.vector.tensor_tensor(tmpb[:, 2], twoi[:, 0:B], twoi[:, 0:B], ALU.mult))
            step(nc.vector.tensor_scalar(tmpb[:, 2], tmpb[:, 2], EPS / down ** 2 / QK_UP ** 2, None, ALU.mult))
            step(nc.vector.tensor_copy(by_unit("eps_u"), column(tmpb[:, 2])))
            step(nc.vector.tensor_scalar(const["o_row"][:], wo_two[:], twoi[:, B:B + 1], 0.5, ALU.mult, ALU.mult))
            step(nc.vector.tensor_scalar(tmpb[:, 1], tmpb[:, 1], two[:, B:B + 1], 2.0 / W_UP, ALU.mult, ALU.mult))
            step(nc.vector.tensor_copy(by_unit("y_scale"), column(tmpb[:, 1])))
            step(nc.vector.tensor_copy(const["taps"][:], smallT[:, 0:B * K].rearrange("p (b c) -> p b c", c=K)))
            step(nc.vector.tensor_scalar(const["taps"][:, B - 1, :], const["taps"][:, B - 1, :], 1.0, None, ALU.add))
            step(nc.vector.tensor_copy(const["conv_b"][:], smallT[:, row_cb:rows]))


def main(nc, const, w_dram, xn_dram, o_dram, x, W_qkv, out):
    B, N, D, K = dims(x, W_qkv)
    U = B * K
    NS = 2 * K
    KH = K // 2
    HC = K // 2
    HW = HC * P
    HN = N // 2
    LEAD = K + 2
    G = NS // 4
    TAPS = B
    H = TAPS - 1
    at = PLAN[K]
    x_t = x.rearrange("b n d -> (b n) d")
    out_t = out.rearrange("b n d -> (b n) d")
    with ExitStack() as ctx:
        def sb(name, shape, dt):
            return ctx.enter_context(nc.sbuf_tensor(name, shape, dt))

        def psum(name, shape, dt):
            return ctx.enter_context(nc.psum_tensor(name, shape, dt))

        def sem(name):
            return ctx.enter_context(nc.semaphore(name))

        w_sb = sb("w_sb", [P, 2, K, 2, 6 * DH], F16)
        xn_sb = sb("xn_sb", [P, 4, K, 2, P], F16)
        stage = sb("stage", [P, 2, 2 * KH, 3 * DH], F32)
        square = sb("square", [P, 4 * KH * DH], F32)
        q_pair = sb("q_pair", [P, 2 * KH, 2 * DH], F16)
        k_pair = sb("k_pair", [P, 2 * KH, 3 * DH], F16)
        stack = sb("stack", [P, 2, 2, 3, N], F16)
        v_pair = sb("v_pair", [P, 2, 2 * K, 2 * DH], F16)
        prob = sb("prob", [P, 4, N], F32)
        p_pair = sb("p_pair", [P, 4, 2, N], F16)
        pT = sb("pT", [P, 4, 2 * K, P], F16)
        o_lo = sb("o_lo", [P, 4, DH], F32)
        o_out = sb("o_out", [P, K, 2, DH], F32)
        y = sb("y", [P, D], F32)
        o_in = sb("o_in", [P, D], F32)
        half = sb("half", [P, HC, P], F32)
        halfx = sb("halfx", [P, HC, P], F32)
        oT = sb("oT", [P, K, 2, P], F16)
        yT = sb("yT", [P, K, H + P], F32)
        acc = sb("acc", [P, K, P], F32)
        fin = sb("fin", [P, D], F32)
        x_in = sb("x_in", [P, D], F32)
        xT = sb("xT", [P, K, 2, P], F16)
        neg = sb("neg", [P, NS], F32)
        bias = sb("bias", [P, NS], F32)
        total = sb("total", [P, 2 * NS], F32)
        inv = sb("inv", [P, 4], F32)
        ms = sb("ms", [P, 4 * KH], F32)
        rs = sb("rs", [P, 4 * KH], F32)
        msx = sb("msx", [P, 4], F32)

        scores = psum("scores", [P, 2, max(N, 1024)], F32)
        values = psum("values", [P, 2, 4, 2 * DH], F32)
        misc = psum("misc", [P, 2, 512], F32)

        gate = sem("gate")
        w_in = [sem(f"w_in{i}") for i in range(2)]
        xn_in = [sem(f"xn_in{i}") for i in range(4)]
        x_ld = sem("x_ld")
        x_sq = sem("x_sq")
        x_ms = sem("x_ms")
        x_pw = sem("x_pw")
        x_hat = sem("x_hat")
        x_tr = sem("x_tr")
        x_ev = sem("x_ev")
        x_hi = sem("x_hi")
        x_lo = sem("x_lo")
        x_mul = sem("x_mul")
        x_st = sem("x_st")
        qkv_mm = sem("qkv_mm")
        qkv_ev = sem("qkv_ev")
        h_sq = sem("h_sq")
        h_ss = sem("h_ss")
        h_ms = sem("h_ms")
        h_pw = sem("h_pw")
        h_n = sem("h_n")
        h_hi = sem("h_hi")
        h_lo = sem("h_lo")
        h_tr = sem("h_tr")
        h_ev = sem("h_ev")
        qk_done = sem("qk_done")
        max_done = sem("max_done")
        bias_done = sem("bias_done")
        exp_done = sem("exp_done")
        hi_done = sem("hi_done")
        lo_done = sem("lo_done")
        pT_in = [sem(f"pT_in{i}") for i in range(4)]
        pv_done = sem("pv_done")
        ov_copy = sem("ov_copy")
        ov_add = sem("ov_add")
        ov_inv = sem("ov_inv")
        ov_done = sem("ov_done")
        o_st = sem("o_st")
        o_ld = sem("o_ld")
        xo_ld = sem("xo_ld")
        o_tr = sem("o_tr")
        o_ev = sem("o_ev")
        o_hi = sem("o_hi")
        o_lo3 = sem("o_lo3")
        s_done = sem("s_done")
        op_mm = sem("op_mm")
        op_ev = sem("op_ev")
        y_tr = sem("y_tr")
        y_ev = sem("y_ev")
        halo = sem("halo")
        cv = sem("cv")
        f_tr = sem("f_tr")
        f_ev = sem("f_ev")
        f_st = sem("f_st")
        block = ctx.enter_context(nc.Block())

        def in_units(eng, unit):
            last_x = U - LEAD

            def pairs(lo, hi, **parts):
                if lo < hi:
                    with eng.Fori(lo // 2, hi // 2) as j:
                        for parity in range(2):
                            unit(2 * j + parity, parity, **parts)

            unit(0, 0, qkv=True, xs=True, outs=False)
            unit(1, 1, qkv=True, xs=True, outs=False)
            pairs(2, K, qkv=True, xs=True, outs=False)
            unit(K, 0, qkv=True, xs=K < last_x, outs=True)
            unit(K + 1, 1, qkv=True, xs=K + 1 < last_x, outs=True)
            pairs(K + 2, last_x, qkv=True, xs=True, outs=True)
            pairs(max(last_x, K + 2), U - 2, qkv=True, xs=False, outs=True)
            unit(U - 2, 0, qkv=True, xs=False, outs=True)
            unit(U - 1, 1, qkv=False, xs=False, outs=True)

        def group(u, s):
            if isinstance(u, int) and NS * u + s < 8:
                return None
            return (G * u + s // 4 - 2, (s // 4) % 2)

        def four(u, s):
            return G * u + s // 4

        def slot(u, s):
            return NS * u + s

        @block.sync
        def _(sp):
            def passed():
                sp.sem_inc(gate, 1)

            def load_x(v):
                need(sp, x_tr, 2 * v)
                sp.dma_start(x_in[:], x_t[bass.ds(v * P, P), :]).then_inc(x_ld, 16)

            def store_xn(v):
                sp.wait_ge(x_hi, 2 * v + 2)
                sp.wait_ge(x_lo, 2 * v + 2)
                sp.dma_start(xn_dram[bass.ds(v, 1)].rearrange("a p n -> (a p) n"),
                             xT[:].rearrange("p c s n -> p (c s n)")).then_inc(x_st, 16)

            def load_w(w, par):
                need(sp, qkv_mm, K * (w - 1))
                sp.dma_start(w_sb[:, par].rearrange("p c s n -> p (c s n)"),
                             w_dram[bass.ds(w % K, 1)].rearrange("a p c s n -> (a p) (c s n)")).then_inc(w_in[par], 16)

            def load_xn(w, t):
                need(sp, qkv_mm, K * w + t - 3)
                need(sp, x_st, 16 * ((w // K) * K + t + 1))
                sp.dma_start(xn_sb[:, t % 4].rearrange("p c s n -> p (c s n)"),
                             xn_dram[bass.ds((w // K) * K + t, 1)].rearrange("a p n -> (a p) n")
                             ).then_inc(xn_in[t % 4], 16)

            def transpose_p(u, s):
                g = slot(u, s)
                sp.wait_ge(lo_done, g + 1)
                passed()
                need(sp, pv_done, g - 3)
                passed()
                sp.dma_start_transpose(pT[:, s % 4], p_pair[:, s % 4].rearrange("p a n -> p (a n)")
                                       ).then_inc(pT_in[s % 4], 16)

            def store_o(u):
                sp.wait_ge(ov_done, G * u + G)
                sp.dma_start(
                    o_dram[bass.ds((u // K) * K * P, K * P), bass.ds((u % K) * P, P)].rearrange(
                        "(t p) n -> p t n", p=P),
                    o_out[:].rearrange("p t h d -> p t (h d)")).then_inc(o_st, 16)

            def load_out(T):
                sp.wait_ge(o_st, 16 * ((T // K) * K + K))
                need(sp, o_tr, 2 * T)
                sp.dma_start(o_in[:], o_dram[bass.ds(T * P, P), :]).then_inc(o_ld, 16)

            def load_xo(T):
                need(sp, y_tr, 2 * T)
                sp.dma_start(y[:], x_t[bass.ds(T * P, P), :]).then_inc(xo_ld, 16)

            def store_out(T):
                sp.wait_ge(f_ev, 2 * T + 2)
                sp.dma_start(out_t[bass.ds(T * P, P), :], fin[:]).then_inc(f_st, 16)

            def unit(u, par, qkv, xs, outs):
                w, v, T = u + 1, u + LEAD, u - K
                for s in range(NS):
                    if qkv and s == 0:
                        for t in range(4):
                            load_xn(w, t)
                    if xs and s == 0:
                        load_x(v)
                    g2 = s - 2
                    if g2 >= 0:
                        transpose_p(u, g2)
                    elif not (isinstance(u, int) and u == 0):
                        transpose_p(u - 1, NS + g2)
                    if qkv and 4 <= s + 3 < K and s >= 1:
                        load_xn(w, s + 3)
                    if qkv and s == K + 1 and not (isinstance(u, int) and u + 2 >= U):
                        load_w(w + 1, 1 - (1 - par))
                    if s == 5 % NS and not (isinstance(u, int) and u == 0):
                        store_o(u - 1)
                    if outs and s == at["ld"]:
                        load_xo(T)
                        if K == 4:
                            pass
                        load_out(T)
                    if xs and s == at["xst"]:
                        store_xn(v)
                if outs:
                    store_out(T)

            load_w(0, 0)
            load_w(1, 1)
            for v in range(LEAD):
                load_x(v)
                if v:
                    store_xn(v - 1)
            store_xn(LEAD - 1)
            for t in range(K):
                load_xn(0, t)
            in_units(sp, unit)
            transpose_p(U - 1, NS - 2)
            transpose_p(U - 1, NS - 1)
            store_o(U - 1)
            with sp.Fori(U - K, U) as T:
                load_xo(T)
                load_out(T)
                store_out(T)
            sp.wait_ge(f_st, 16 * U)

        @block.tensor
        def _(pe):
            def bank(i):
                return misc[:, i]

            def f16_bank(i):
                return misc[:, i].bitcast(F16).rearrange("p (a n) -> p a n", a=2)

            def qk(u, s, par):
                h, qt = s // K, s % K
                need(pe, exp_done, slot(u, s) - 1)
                for n in range(2):
                    for i in range(2):
                        last = nc.tensor.matmul(scores[:, s % 2, n * HN:(n + 1) * HN],
                                                stack[:, par, h, 0, qt * P:(qt + 1) * P],
                                                stack[:, par, h, 1 + i, n * HN:(n + 1) * HN],
                                                start=(i == 0), stop=(i == 1))
                last.then_inc(qk_done, 1)

            def pv(u, s, par):
                h = s // K
                g = slot(u, s)
                if s % 4 == 0:
                    need(pe, ov_done, four(u, s) - 1)
                pe.wait_ge(pT_in[s % 4], 16 * (four(u, s) + 1))
                o = values[:, (s // 4) % 2, s % 4, :]
                for t in range(K - 1):
                    nc.tensor.matmul(o, pT[:, s % 4, t, :], v_pair[:, par, 2 * t + h, :],
                                     start=(t == 0), stop=False)
                for t in range(K):
                    nc.tensor.matmul(o[:, 0:DH], pT[:, s % 4, K + t, :], v_pair[:, par, 2 * t + h, 0:DH],
                                     start=False, stop=False)
                last = nc.tensor.matmul(o, pT[:, s % 4, K - 1, :], v_pair[:, par, 2 * (K - 1) + h, :],
                                        start=False, stop=True)
                last.then_inc(pv_done, 1)

            def project(w, par, t):
                if t == 0:
                    pe.wait_ge(w_in[par], 8 * (w - par) + 16)
                else:
                    pass
                if t >= 2:
                    pe.wait_ge(qkv_ev, K * w + t - 1)
                pe.wait_ge(xn_in[t % 4], 16 * (K // 4 * w + t // 4 + 1))
                acc_ = bank(t % 2)[:, 0:6 * DH]
                for c in range(K):
                    for i, j in ((0, 0), (0, 1), (1, 0)):
                        last = nc.tensor.matmul(acc_, xn_sb[:, t % 4, c, i, :], w_sb[:, par, c, j, :],
                                                start=(c == 0 and i == j == 0), stop=(c == K - 1 and i == 1))
                last.then_inc(qkv_mm, 1)

            def stacks(w, hf, before):
                pe.wait_ge(h_lo, 3 * (2 * w + hf) + 2)
                pe.wait_ge(h_hi, 3 * (2 * w + hf) + 2)
                for i, b in enumerate((0, 1, 0)):
                    need(pe, *before[i])
                    for t in range(KH):
                        for a in range(2):
                            src = ((q_pair[:, 2 * t + i, :] if a == 0 else k_pair[:, 2 * t + i, 0:2 * DH])
                                   if i < 2 else k_pair[:, 2 * t + a, DH:3 * DH])
                            last = nc.tensor.transpose(f16_bank(b)[:, a, t * P:(t + 1) * P], src, const["eye16"][:])
                    last.then_inc(h_tr, 1)

            def x_transposes(v, before):
                pe.wait_ge(x_hat, v + 1)
                for hh, b in enumerate((1, 0)):
                    need(pe, *before[hh])
                    for c in range(HC):
                        last = nc.tensor.transpose(bank(b)[:, c * P:(c + 1) * P],
                                                   x_in[:, (hh * HC + c) * P:(hh * HC + c + 1) * P], const["eye32"][:])
                    last.then_inc(x_tr, 1)

            def o_transposes(T, before):
                pe.wait_ge(o_ld, 16 * (T + 1))
                for hh, b in enumerate((1, 0)):
                    need(pe, *before[hh])
                    for c in range(HC):
                        last = nc.tensor.transpose(bank(b)[:, c * P:(c + 1) * P],
                                                   o_in[:, (hh * HC + c) * P:(hh * HC + c + 1) * P], const["eye32"][:])
                    last.then_inc(o_tr, 1)

            def out_product(T, n, part, parts, before):
                if part == 0:
                    pe.wait_ge(o_hi, 2 * T + 2)
                    pe.wait_ge(o_lo3, 2 * T + 2)
                    need(pe, *before)
                for c in range(part * K // parts, (part + 1) * K // parts):
                    for i, j in ((0, 0), (0, 1), (1, 0)):
                        last = nc.tensor.matmul(bank(1)[:, 0:HN], oT[:, c, i, :], const["wo"][:, c, j, n * HN:(n + 1) * HN],
                                                start=(c == 0 and i == j == 0), stop=(c == K - 1 and i == 1))
                if part == parts - 1:
                    last.then_inc(op_mm, 1)

            def y_transposes(T, hh, before):
                pe.wait_ge(op_ev, 2 * T + hh + 1)
                need(pe, *before)
                for c in range(HC):
                    last = nc.tensor.transpose(bank(hh)[:, c * P:(c + 1) * P],
                                               y[:, (hh * HC + c) * P:(hh * HC + c + 1) * P], const["eye32"][:])
                last.then_inc(y_tr, 1)

            def out_transposes(T):
                for hh in range(2):
                    pe.wait_ge(cv, TAPS * K * T + TAPS * HC * (hh + 1))
                    pe.wait_ge(y_ev, 2 * T + hh + 1)
                    for c in range(HC):
                        last = nc.tensor.transpose(bank(hh)[:, c * P:(c + 1) * P], acc[:, hh * HC + c, :],
                                                   const["eye32"][:])
                    last.then_inc(f_tr, 1)

            def unit(u, par, qkv, xs, outs):
                w, v, T = u + 1, u + LEAD, u - K
                for s in range(NS):
                    if s == 0:
                        pe.wait_ge(h_ev, 6 * (u + 1))
                        if outs:
                            need(pe, f_ev, 2 * T)
                    qk(u, s, par)
                    if qkv and s < K:
                        project(w, 1 - par, s)
                    if qkv and s == at["th0"]:
                        stacks(w, 0, ((qkv_ev, K * w + K - 1), (qkv_ev, K * w + K), (h_ev, 6 * w + 1)))
                    if outs and s == at["ot"]:
                        o_transposes(T, ((h_ev, 6 * w + 2), (h_ev, 6 * w + 3)) if qkv else ((f_ev, 2 * T),) * 2)
                    if xs and s == at["xt"]:
                        x_transposes(v, ((o_ev, 2 * T + 1), (o_ev, 2 * T + 2)) if outs else
                                     ((h_ev, 6 * w + 2), (h_ev, 6 * w + 3)))
                    if s >= LAG:
                        pv(u, s - LAG, par)
                    elif not (isinstance(u, int) and u == 0):
                        pv(u - 1, NS + s - LAG, 1 - par)
                    if outs and s == at["op0a"]:
                        out_product(T, 0, 0, 2, (x_ev, 2 * v + 1) if xs else (o_ev, 2 * T + 1))
                    if outs and s == at["op0b"]:
                        out_product(T, 0, 1, 2, None)
                    if qkv and s == at["th1"]:
                        b0 = (x_ev, 2 * v + 2) if xs else (o_ev, 2 * T + 2)
                        b1 = (op_ev, 2 * T + 1) if outs else (x_ev, 2 * v + 1)
                        stacks(w, 1, (b0, b1, (h_ev, 6 * w + 4)))
                    if outs and s == at["op1a"]:
                        out_product(T, 1, 0, 2, (h_ev, 6 * w + 5) if qkv else (op_ev, 2 * T + 1))
                    if outs and s == at["op1b"]:
                        out_product(T, 1, 1, 2, None)
                    if outs and s == at["yt0"]:
                        y_transposes(T, 0, (h_ev, 6 * w + 6) if qkv else (o_ev, 2 * T + 2))
                    if outs and s == at["yt1"]:
                        y_transposes(T, 1, (op_ev, 2 * T + 2))
                    if outs and s == at["fin"]:
                        out_transposes(T)

            for v in range(LEAD):
                x_transposes(v, ((x_ev, 2 * v - 1), (x_ev, 2 * v)))
            pe.wait_ge(x_ev, 2 * LEAD)
            for t in range(K):
                project(0, 0, t)
                if t == KH + 1:
                    pass
            stacks(0, 0, ((qkv_ev, K - 1), (qkv_ev, K), (h_ev, 1)))
            stacks(0, 1, ((h_ev, 3), (h_ev, 2), (h_ev, 4)))
            in_units(pe, unit)
            for s in range(NS - LAG, NS):
                pv(U - 1, s, 1)
            with pe.Fori(U - K, U) as T:
                o_transposes(T, ((f_ev, 2 * T), (f_ev, 2 * T)))
                out_product(T, 0, 0, 1, (o_ev, 2 * T + 1))
                out_product(T, 1, 0, 1, (op_ev, 2 * T + 1))
                y_transposes(T, 0, (o_ev, 2 * T + 2))
                y_transposes(T, 1, (op_ev, 2 * T + 2))
                out_transposes(T)

        @block.scalar
        def _(act):
            def exponent(u, s, par):
                g = slot(u, s)
                act.wait_ge(bias_done, g + 1)
                need(act, lo_done, g - 3)
                if s % 4 == 0:
                    need(act, ov_inv, four(u, s) - 7)
                nc.scalar.activation(prob[:, s % 4, :], scores[:, s % 2, 0:N], ACT.Exp, bias=bias[:, s:s + 1],
                                     scale=const["l_scale"][:, 0:1],
                                     accum_out=total[:, par * NS + s:par * NS + s + 1]).then_inc(exp_done, 1)

            def read_projection(w, t):
                hf = t // KH
                act.wait_ge(qkv_mm, K * w + t + 1)
                if t % KH == 0:
                    need(act, h_lo, 3 * (2 * (w - 1) + hf + 1))
                nc.scalar.activation(stage[:, hf, 2 * (t % KH):2 * (t % KH) + 2, :],
                                     misc[:, t % 2, 0:6 * DH].rearrange("p (h n) -> p h n", h=2), ACT.Copy,
                                     scale=QKV_DOWN).then_inc(qkv_ev, 1)

            def squares(w, hf):
                act.wait_ge(qkv_ev, K * w + (hf + 1) * KH)
                need(act, h_ss, 2 * w + hf)
                nc.scalar.activation(square[:].rearrange("p (t n) -> p t n", n=2 * DH),
                                     stage[:, hf, :, 0:2 * DH], ACT.Square).then_inc(h_sq, 1)

            def high_halves(w, par, hf):
                act.wait_ge(h_n, 2 * (2 * w + hf) + 2)
                need(act, h_tr, 3 * (2 * w + hf))
                nc.scalar.activation(q_pair[:, :, 0:DH], stage[:, hf, :, 0:DH], ACT.Copy).then_inc(h_hi, 1)
                kk = k_pair[:].rearrange("p t (a d) -> p t a d", d=DH)
                for a in (0, 2):
                    last = nc.scalar.activation(kk[:, :, a, :], stage[:, hf, :, DH:2 * DH], ACT.Copy)
                last.then_inc(h_hi, 1)
                need(act, pv_done, NS * (w - 1))
                nc.scalar.activation(v_pair[:, par, 2 * KH * hf:2 * KH * (hf + 1), 0:DH],
                                     stage[:, hf, :, 2 * DH:3 * DH], ACT.Copy).then_inc(h_hi, 1)

            def read_stacks(w, par, hf):
                for i, b in enumerate((0, 1, 0)):
                    act.wait_ge(h_tr, 3 * (2 * w + hf) + i + 1)
                    dst = stack[:, par, i, 0:2, hf * HN:(hf + 1) * HN] if i < 2 else \
                        stack[:, par, :, 2, hf * HN:(hf + 1) * HN]
                    nc.scalar.activation(dst, misc[:, b].bitcast(F16).rearrange("p (a n) -> p a n", a=2)[:, :, 0:HN],
                                         ACT.Copy).then_inc(h_ev, 1)

            def x_square(v, ss_count):
                act.wait_ge(x_ld, 16 * (v + 1))
                need(act, h_ss, ss_count)
                need(act, x_ms, v)
                nc.scalar.activation(square[:, 0:D].bitcast(F16)[:, 0:D], x_in[:], ACT.Square,
                                     accum_out=msx[:, 0:1]).then_inc(x_sq, 1)

            def x_scale(v):
                act.wait_ge(x_pw, v + 1)
                nc.scalar.activation(x_in[:], x_in[:], ACT.Copy, scale=msx[:, 2:3]).then_inc(x_hat, 1)

            def x_high(v):
                for hh in range(2):
                    act.wait_ge(x_ev, 2 * v + hh + 1)
                    need(act, x_st, 16 * v)
                    nc.scalar.activation(xT[:, hh * HC:(hh + 1) * HC, 0, :], halfx[:], ACT.Copy).then_inc(x_hi, 1)

            def read_values_low(q):
                count, b = q
                act.wait_ge(pv_done, 4 * count + 4)
                need(act, ov_done, count)
                nc.scalar.activation(o_lo[:], values[:, b, :, DH:2 * DH], ACT.Copy).then_inc(ov_copy, 1)

            def o_high(T):
                for hh in range(2):
                    act.wait_ge(o_ev, 2 * T + hh + 1)
                    need(act, op_mm, 2 * T)
                    nc.scalar.activation(oT[:, hh * HC:(hh + 1) * HC, 0, :], half[:], ACT.Copy).then_inc(o_hi, 1)

            def read_yT(T, hh):
                act.wait_ge(y_tr, 2 * T + hh + 1)
                act.wait_ge(halo, T + 1)
                nc.scalar.activation(yT[:, hh * HC:(hh + 1) * HC, H:H + P],
                                     misc[:, hh, 0:HW].rearrange("p (c n) -> p c n", n=P), ACT.Copy).then_inc(y_ev, 1)

            def read_out(T):
                need(act, f_st, 16 * T)
                for hh in range(2):
                    act.wait_ge(f_tr, 2 * T + hh + 1)
                    nc.scalar.activation(fin[:, hh * HW:(hh + 1) * HW], misc[:, hh, 0:HW], ACT.Copy).then_inc(f_ev, 1)

            def unit(u, par, qkv, xs, outs):
                w, v, T = u + 1, u + LEAD, u - K
                for s in range(NS):
                    exponent(u, s, par)
                    if s % 4 == 0:
                        q = group(u, s)
                        if q:
                            read_values_low(q)
                    if qkv and s < K:
                        read_projection(w, s)
                    if qkv and s == at["te0"]:
                        read_stacks(w, 1 - par, 0)
                    if outs and s == at["ohi"]:
                        o_high(T)
                    if xs and s == at["xhi"]:
                        x_high(v)
                    if qkv and s == at["te1"]:
                        read_stacks(w, 1 - par, 1)
                    if xs and s == at["xs"]:
                        x_square(v, 2 * w)
                    if xs and s == at["xh"]:
                        x_scale(v)
                    for hf in range(2):
                        if qkv and s == at[f"sq{hf}"]:
                            squares(w, hf)
                        if qkv and s == at[f"hi{hf}"]:
                            high_halves(w, 1 - par, hf)
                    if outs and s == at["ye0"]:
                        read_yT(T, 0)
                    if outs and s == at["ye1"]:
                        read_yT(T, 1)
                    if outs and s == at["fin"]:
                        read_out(T)

            for v in range(LEAD):
                x_square(v, 0)
                x_scale(v)
                x_high(v)
            for hf in range(2):
                for t in range(KH * hf, KH * (hf + 1)):
                    read_projection(0, t)
                squares(0, hf)
            for hf in range(2):
                high_halves(0, 0, hf)
                read_stacks(0, 0, hf)
            in_units(act, unit)
            for i in range(2):
                read_values_low((G * U - 2 + i, i))
            with act.Fori(U - K, U) as T:
                o_high(T)
                read_yT(T, 0)
                read_yT(T, 1)
                read_out(T)

        @block.gpsimd
        def _(pool):
            def low(u, s):
                pool.wait_ge(hi_done, slot(u, s) + 1)
                nc.gpsimd.tensor_tensor(p_pair[:, s % 4, 1, :], prob[:, s % 4, :], p_pair[:, s % 4, 0, :],
                                        ALU.subtract).then_inc(lo_done, 1)

            def half_power(w, hf):
                pool.wait_ge(h_ms, 2 * w + hf + 1)
                need(pool, h_n, 2 * (2 * w + hf))
                nc.gpsimd.tensor_tensor(rs[:], ms[:], const["power"][:, 0:4 * KH], ALU.pow).then_inc(h_pw, 1)

            def half_low(w, par, hf):
                n = 2 * w + hf
                pool.wait_ge(h_hi, 3 * n + 3)
                nc.gpsimd.tensor_tensor(q_pair[:, :, DH:2 * DH], stage[:, hf, :, 0:DH], q_pair[:, :, 0:DH],
                                        ALU.subtract).then_inc(h_lo, 1)
                nc.gpsimd.tensor_tensor(k_pair[:, :, DH:2 * DH], stage[:, hf, :, DH:2 * DH], k_pair[:, :, 0:DH],
                                        ALU.subtract).then_inc(h_lo, 1)
                vp = v_pair[:, par, 2 * KH * hf:2 * KH * (hf + 1), :]
                nc.gpsimd.tensor_tensor(vp[:, :, DH:2 * DH], stage[:, hf, :, 2 * DH:3 * DH], vp[:, :, 0:DH],
                                        ALU.subtract).then_inc(h_lo, 1)

            def x_power(v):
                pool.wait_ge(x_ms, v + 1)
                need(pool, x_hat, v)
                nc.gpsimd.tensor_tensor(msx[:, 2:3], msx[:, 1:2], const["power"][:, 0:1], ALU.pow).then_inc(x_pw, 1)

            def x_low(v):
                for hh in range(2):
                    pool.wait_ge(x_hi, 2 * v + hh + 1)
                    nc.gpsimd.tensor_tensor(xT[:, hh * HC:(hh + 1) * HC, 1, :], halfx[:],
                                            xT[:, hh * HC:(hh + 1) * HC, 0, :], ALU.subtract).then_inc(x_lo, 1)

            def o_low(T):
                for hh in range(2):
                    pool.wait_ge(o_hi, 2 * T + hh + 1)
                    nc.gpsimd.tensor_tensor(oT[:, hh * HC:(hh + 1) * HC, 1, :], half[:],
                                            oT[:, hh * HC:(hh + 1) * HC, 0, :], ALU.subtract).then_inc(o_lo3, 1)

            def unit(u, par, qkv, xs, outs):
                w, v, T = u + 1, u + LEAD, u - K
                for s in range(NS):
                    if s:
                        low(u, s - 1)
                    elif not (isinstance(u, int) and u == 0):
                        low(u - 1, NS - 1)
                    if outs and s == at["olo"]:
                        o_low(T)
                    if xs and s == at["xlo"]:
                        x_low(v)
                    if xs and s == at["xs"]:
                        x_power(v)
                    for hf in range(2):
                        if qkv and s == at[f"ss{hf}"]:
                            half_power(w, hf)
                        if qkv and s == at[f"lo{hf}"]:
                            half_low(w, 1 - par, hf)

            for v in range(LEAD):
                x_power(v)
                x_low(v)
            for hf in range(2):
                half_power(0, hf)
                half_low(0, 0, hf)
            in_units(pool, unit)
            low(U - 1, NS - 1)
            with pool.Fori(U - K, U) as T:
                o_low(T)

        @block.vector
        def _(dve):
            def maximum(u, s):
                g = slot(u, s)
                dve.wait_ge(qk_done, g + 1)
                nc.vector.tensor_reduce(neg[:, s:s + 1], scores[:, s % 2, 0:N], axis=AX.X, op=ALU.max,
                                        negate=True).then_inc(max_done, 1)
                dve.wait_ge(max_done, g + 1)
                nc.vector.tensor_scalar(bias[:, s:s + 1], neg[:, s:s + 1], const["l_scale"][:, 0:1], P_SHIFT,
                                        ALU.mult, ALU.add).then_inc(bias_done, 1)

            def high(u, s):
                g = slot(u, s)
                dve.wait_ge(exp_done, g + 1)
                need(dve, pT_in[s % 4], 16 * four(u, s))
                nc.vector.tensor_copy(p_pair[:, s % 4, 0, :], prob[:, s % 4, :]).then_inc(hi_done, 1)

            def sums(w, hf):
                n = 2 * w + hf
                dve.wait_ge(h_sq, n + 1)
                nc.vector.tensor_reduce(ms[:], square[:].rearrange("p (t d) -> p t d", d=DH), axis=AX.X,
                                        op=ALU.add).then_inc(h_ss, 1)
                dve.wait_ge(h_ss, n + 1)
                nc.vector.tensor_scalar(ms[:], ms[:], 1.0 / (DH * QK_UP ** 2), const["eps_u"][:, bass.ds(w, 1)],
                                        ALU.mult, ALU.add).then_inc(h_ms, 1)

            def normalise(w, hf):
                n = 2 * w + hf
                dve.wait_ge(h_pw, n + 1)
                qk_ = stage[:, hf, :, 0:2 * DH].rearrange("p t (j d) -> p t j d", d=DH)
                r_ = rs[:].rearrange("p (t j a) -> p t j a", j=2, a=1).to_broadcast([P, 2 * KH, 2, DH])
                nc.vector.tensor_tensor(qk_, qk_, r_, ALU.mult).then_inc(h_n, 1)
                dve.wait_ge(h_n, 2 * n + 1)
                q_ = stage[:, hf, :, 0:DH]
                g_ = const["g_qk"][:].rearrange("p (a d) -> p a d", a=1).to_broadcast([P, 2 * KH, DH])
                nc.vector.tensor_tensor(q_, q_, g_, ALU.mult).then_inc(h_n, 1)

            def x_mean(v):
                dve.wait_ge(x_sq, v + 1)
                need(dve, x_pw, v)
                nc.vector.tensor_scalar(msx[:, 1:2], msx[:, 0:1], 1.0 / D, EPS, ALU.mult, ALU.add).then_inc(x_ms, 1)

            def x_modulate(v):
                for hh, b in enumerate((1, 0)):
                    dve.wait_ge(x_tr, 2 * v + hh + 1)
                    need(dve, x_lo, 2 * v + hh)

                    def mod(name):
                        m = const[name][:, bass.ds(v, 1), hh * HC:(hh + 1) * HC]
                        return m.rearrange("p a (c b) -> p (a c) b", b=1).to_broadcast([P, HC, P])

                    nc.vector.tensor_tensor(halfx[:], misc[:, b, 0:HW].rearrange("p (c n) -> p c n", n=P),
                                            mod("mod_a"), ALU.mult).then_inc(x_mul, 1)
                    dve.wait_ge(x_mul, 2 * v + hh + 1)
                    nc.vector.tensor_tensor(halfx[:], halfx[:], mod("mod_s"), ALU.add).then_inc(x_ev, 1)

            def read_values(q, tile, head, col):
                count, b = q
                dve.wait_ge(exp_done, 4 * count + 4)
                nc.vector.reciprocal(inv[:], total[:, col:col + 4]).then_inc(ov_inv, 1)
                dve.wait_ge(ov_copy, count + 1)
                nc.vector.tensor_tensor(o_lo[:], values[:, b, :, 0:DH], o_lo[:], ALU.add).then_inc(ov_add, 1)
                dve.wait_ge(ov_add, count + 1)
                nc.vector.tensor_tensor(
                    o_out[:, tile:tile + 4, head, :], o_lo[:],
                    inv[:].rearrange("p (t a) -> p t a", a=1).to_broadcast([P, 4, DH]), ALU.mult).then_inc(ov_done, 1)

            def values_at(u, s, par):
                q = group(u, s)
                if not q:
                    return
                first = (s - 8) % NS
                upar = par if s >= 8 else 1 - par
                if first == 0:
                    need(dve, o_st, 16 * (u if s >= 8 else u - 1))
                dve_read(q, first, upar)

            def dve_read(q, first, upar):
                need(dve, ov_done, q[0])
                read_values(q, first % K, first // K, upar * NS + first)

            def residual(T):
                dve.wait_ge(xo_ld, 16 * (T + 1))
                dve.wait_ge(o_ld, 16 * (T + 1))
                nc.vector.scalar_tensor_tensor(out=y[:], in0=o_in[:], scalar=const["v_scale"][:, bass.ds(T, 1)],
                                               in1=y[:], op0=ALU.mult, op1=ALU.add).then_inc(s_done, 1)

            def o_scale(T):
                for hh, b in enumerate((1, 0)):
                    dve.wait_ge(o_tr, 2 * T + hh + 1)
                    need(dve, o_lo3, 2 * T + hh)
                    m = const["o_row"][:, hh * HC:(hh + 1) * HC].rearrange("p (c b) -> p c b", b=1)
                    nc.vector.tensor_tensor(half[:], misc[:, b, 0:HW].rearrange("p (c n) -> p c n", n=P),
                                            m.to_broadcast([P, HC, P]), ALU.mult).then_inc(o_ev, 1)

            def add_product(T, n):
                dve.wait_ge(op_mm, 2 * T + n + 1)
                dve.wait_ge(s_done, T + 1)
                ys = y[:, n * HN:(n + 1) * HN]
                nc.vector.scalar_tensor_tensor(out=ys, in0=misc[:, 1, 0:HN], scalar=const["y_scale"][:, bass.ds(T, 1)],
                                               in1=ys, op0=ALU.mult, op1=ALU.add).then_inc(op_ev, 1)

            def carry_tokens(T):
                need(dve, cv, TAPS * K * T)
                nc.vector.tensor_scalar(yT[:, :, 0:H], yT[:, :, P:P + H], const["carry"][:, bass.ds(T, 1)], None,
                                        ALU.mult).then_inc(halo, 1)

            def convolve(T, hh):
                dve.wait_ge(y_ev, 2 * T + hh + 1)
                need(dve, f_tr, 2 * T)
                base = TAPS * K * T + TAPS * HC * hh
                for k in range(TAPS - 1, -1, -1):
                    for i in range(HC):
                        c = hh * HC + i
                        if k == TAPS - 1:
                            nc.vector.tensor_scalar(acc[:, c, :], yT[:, c, k:k + P], const["taps"][:, k, c:c + 1],
                                                    const["conv_b"][:, c:c + 1], ALU.mult, ALU.add).then_inc(cv, 1)
                        else:
                            dve.wait_ge(cv, base + HC * (TAPS - 2 - k) + i + 1)
                            nc.vector.scalar_tensor_tensor(out=acc[:, c, :], in0=yT[:, c, k:k + P],
                                                           scalar=const["taps"][:, k, c:c + 1], in1=acc[:, c, :],
                                                           op0=ALU.mult, op1=ALU.add).then_inc(cv, 1)

            def unit(u, par, qkv, xs, outs):
                w, v, T = u + 1, u + LEAD, u - K
                for s in range(NS):
                    maximum(u, s)
                    if s:
                        high(u, s - 1)
                    elif not (isinstance(u, int) and u == 0):
                        high(u - 1, NS - 1)
                    if s % 4 == 0:
                        values_at(u, s, par)
                    if outs and s == at["s"]:
                        residual(T)
                    if outs and s == at["oe"]:
                        o_scale(T)
                    if xs and s == at["xe"]:
                        x_modulate(v)
                    if xs and s == at["xs"]:
                        x_mean(v)
                    for hf in range(2):
                        if qkv and s == at[f"ss{hf}"]:
                            sums(w, hf)
                        if qkv and s == at[f"n{hf}"]:
                            normalise(w, hf)
                    if outs and s == at["y0"]:
                        add_product(T, 0)
                        carry_tokens(T)
                    if outs and s == at["y1"]:
                        add_product(T, 1)
                    if outs and s == at["cv0"]:
                        convolve(T, 0)
                    if outs and s == at["cv1"]:
                        convolve(T, 1)

            nc.vector.memset(yT[:], 0.0)
            for v in range(LEAD):
                x_mean(v)
                x_modulate(v)
            for hf in range(2):
                sums(0, hf)
                normalise(0, hf)
            in_units(dve, unit)
            high(U - 1, NS - 1)
            for i in range(2):
                dve_read((G * U - 2 + i, i), NS - 8 + 4 * i, 1)
            with dve.Fori(U - K, U) as T:
                residual(T)
                o_scale(T)
                add_product(T, 0)
                carry_tokens(T)
                add_product(T, 1)
                convolve(T, 0)
                convolve(T, 1)


_INS = ["x", "cond_2048", "L0_cond_W_emb", "L0_cond_b_emb", "L0_cond_g_norm", "L0_cond_W_qkv",
        "L0_cond_g_q", "L0_cond_g_k", "L0_cond_W_out", "L1_cond_b"]


def kernel(**inputs):
    import numpy as _np
    import concourse.bacc as _bacc
    from concourse import mybir as _mybir
    from concourse.bass_utils import run_bass_kernel_spmd as _run

    nc = _bacc.Bacc("TRN2", target_bir_lowering=False, num_devices=1, dynamic_dma_scratch_size=1024)
    arrays, args = {}, []
    for name in _INS:
        a = _np.ascontiguousarray(inputs[name])
        arrays[f"in_{name}"] = a
        args.append(nc.dram_tensor(f"in_{name}", a.shape, _mybir.dt.from_np(a.dtype), kind="ExternalInput").ap())
    args.append(nc.dram_tensor("out_0", inputs["x"].shape, _mybir.dt.float32, kind="ExternalOutput").ap())
    bass_cond_attention_conv(nc, *args)
    r = _run(nc, [arrays], core_ids=[0])
    return r.results[0]["out_0"]
```

```python
from contextlib import ExitStack

import numpy as np

import concourse.bass as bass
from concourse import mybir

P = 128
F32 = mybir.dt.float32
F16 = mybir.dt.float16
U32 = mybir.dt.uint32
I32 = mybir.dt.int32
ALU = mybir.AluOpType
ACT = mybir.ActivationFunctionType
AX = mybir.AxisListType
RMAX = bass.bass_isa.ReduceOp.max

EPS = 1e-6
DH = 64
LAG = 4
X_UP = 256.0
W_UP = 1024.0
QKV_DOWN = 2.0 ** -16
QK_UP = 64.0
P_SHIFT = 12 * float(np.log(2.0))
EXPONENT = 0x7F800000
TINY = 1e-30

PLAN = {
    8: dict(xs=2, xh=3, cv=(0, 1, 2, 3), fin=4, st=6,
            sq0=4, ss0=4, n0=5, hi0=5, lo0=6, h00=7, h01=8, h02=8,
            sq1=8, ss1=8, n1=9, hi1=10, lo1=11, h10=12, h11=13, h12=14,
            ld=6, res=8, ot=9, ohi=10, olo=10, xt=10, xhi=11, xlo=12, xst=14,
            op0a=11, op0b=12, op1a=13, op1b=14, yt=15),
    4: dict(xs=1, xh=1, cv=(0, 0, 1, 1), fin=2, st=3,
            sq0=2, ss0=2, n0=2, hi0=3, lo0=3, h00=3, h01=4, h02=4,
            sq1=4, ss1=4, n1=4, hi1=4, lo1=4, h10=6, h11=7, h12=7,
            ld=5, res=5, ot=5, ohi=5, olo=5, xt=5, xhi=6, xlo=6, xst=6,
            op0a=6, op0b=6, op1a=7, op1b=7, yt=7),
}


def need(eng, sem, count):
    if isinstance(count, int) and count <= 0:
        return
    eng.wait_ge(sem, count)


def dims(x, W_qkv):
    B, N, D = x.shape
    K = D // P
    assert N == D and K in PLAN and W_qkv.shape == (D, 3 * D)
    return B, N, D, K


def bass_cond_attention_conv(nc, x, cond, W_emb, b_emb, g_norm, W_qkv, g_q, g_k, W_out, b_conv, out):
    B, N, D, K = dims(x, W_qkv)
    U = B * K
    with ExitStack() as ctx:
        def sb(name, shape, dt):
            return ctx.enter_context(nc.sbuf_tensor(name, shape, dt))

        const = dict(
            eye32=sb("eye32", [P, P], F32), eye16=sb("eye16", [P, P], F16),
            wo=sb("wo", [P, K, 2, D], F16),
            mod_a=sb("mod_a", [P, U, K], F32),
            mod_s=sb("mod_s", [P, U, K], F32),
            eps_u=sb("eps_u", [P, U], F32),
            v_scale=sb("v_scale", [P, U], F32),
            y_scale=sb("y_scale", [P, U], F32),
            carry=sb("carry", [P, U], F32),
            o_row=sb("o_row", [P, K], F32),
            g_qk=sb("g_qk", [P, DH], F32),
            l_scale=sb("l_scale", [P, 1], F32),
            taps=sb("taps", [P, B, K], F32), conv_b=sb("conv_b", [P, K], F32),
            power=sb("power", [P, 4 * K], F32),
        )
        w_dram = nc.dram_tensor("w_dram", [K, P, K, 2, 6 * DH], F16, kind="Internal").ap()
        xn_dram = nc.dram_tensor("xn_dram", [U, P, K * 2 * P], F16, kind="Internal").ap()
        o_dram = nc.dram_tensor("o_dram", [U * P, D], F32, kind="Internal").ap()
        prepare(nc, const, w_dram, x, cond, W_emb, b_emb, g_norm, W_qkv, g_q, g_k, W_out, b_conv)
        main(nc, const, w_dram, xn_dram, o_dram, x, W_qkv, out)


def prepare(nc, const, w_dram, x, cond, W_emb, b_emb, g_norm, W_qkv, g_q, g_k, W_out, b_conv):
    B, N, D, K = dims(x, W_qkv)
    NE = 2 * D // 512
    rows = B * K + 4 * K
    row_embb, row_g, row_cb = B * K, B * K + 2 * K, B * K + 3 * K
    with ExitStack() as ctx:
        def sb(name, shape, dt):
            return ctx.enter_context(nc.sbuf_tensor(name, shape, dt))

        def psum(name, shape, dt):
            return ctx.enter_context(nc.psum_tensor(name, shape, dt))

        def sem(name):
            return ctx.enter_context(nc.semaphore(name))

        small = sb("small", [rows, P], F32)
        smallT = sb("smallT", [P, rows], F32)
        emb_w = sb("emb_w", [P, 2, 2 * D], F32)
        wq_raw = sb("wq_raw", [P, 3, 3 * D], F32)
        wq_pair = sb("wq_pair", [P, 2, K, 2, 6 * DH], F16)
        wo_raw = sb("wo_raw", [P, 2, D], F32)
        ss_row = sb("ss_row", [B, 2 * D], F32)
        ssT = sb("ssT", [P, 2 * K, B], F32)
        mod = sb("mod", [P, 2, K, B], F32)
        wide = sb("wide", [P, 2, K, B], F32)
        gq = sb("gq", [P, 2, DH], F32)
        wq_max = sb("wq_max", [P, K], F32)
        wq_two = sb("wq_two", [P, K], F32)
        wq_inv = sb("wq_inv", [P, K], F32)
        wo_max = sb("wo_max", [P, K], F32)
        wo_two = sb("wo_two", [P, K], F32)
        wo_inv = sb("wo_inv", [P, K], F32)
        top = sb("top", [P, B + 1], F32)
        topr = sb("topr", [P, B + 1], F32)
        two = sb("two", [P, B + 1], F32)
        twoi = sb("twoi", [P, B + 1], F32)
        gmax = sb("gmax", [P, 4], F32)
        tmpb = sb("tmpb", [P, 3, B], F32)
        ps_row = psum("ps_row", [B, 2 * D], F32)
        ps_t = psum("ps_t", [P, 512], F32)
        ps_s = psum("ps_s", [P, 512], F32)

        small_in = sem("small_in")
        g_in = sem("g_in")
        emb_in = [sem(f"emb_in{i}") for i in range(2)]
        wq_in = [sem(f"wq_in{i}") for i in range(3)]
        wo_in = [sem(f"wo_in{i}") for i in range(2)]
        wq_out = [sem(f"wq_out{i}") for i in range(2)]
        eye = sem("eye")
        eyed = sem("eyed")
        small_t = sem("small_t")
        small_c = sem("small_c")
        emb_mm = sem("emb_mm")
        emb_row = sem("emb_row")
        emb_t = sem("emb_t")
        dve = sem("dve_step")
        wq_scaled = sem("wq_scaled")
        wq_hi = sem("wq_hi")
        wq_lo = sem("wq_lo")
        wo_scaled = sem("wo_scaled")
        wo_hi = sem("wo_hi")
        wo_lo = sem("wo_lo")
        top_in = sem("top_in")
        top_all = sem("top_all")
        emb_v = W_emb.rearrange("(c p) n -> c p n", p=P)
        wq_v = W_qkv.rearrange("(c p) n -> c p n", p=P)
        wo_v = W_out.rearrange("(c p) n -> c p n", p=P)
        block = ctx.enter_context(nc.Block())

        def store_wq(sp, c):
            sp.wait_ge(wq_hi, 3 * (c + 1))
            sp.wait_ge(wq_lo, c + 1)
            sp.dma_start(w_dram[:, :, c].rearrange("h p s n -> p h (s n)"),
                         wq_pair[:, c % 2].rearrange("p h s n -> p h (s n)")).then_inc(wq_out[c % 2], 16)

        def by_head(c, s, j):
            return wq_pair[:, c % 2, :, s, :].rearrange("p g (h j d) -> p g h j d", h=2, j=3)[:, :, :, j, :]

        def raw_by_head(c, j):
            return wq_raw[:, c % 3, j * D:(j + 1) * D].rearrange("p (g h d) -> p g h d", h=2, d=DH)

        @block.sync
        def _(sp):
            sp.dma_start(small[0:B * K, :], cond.rearrange("b (c p) -> (b c) p", p=P)).then_inc(small_in, 16)
            sp.dma_start(small[row_embb:row_g, :], b_emb.rearrange("(c p) -> c p", p=P)).then_inc(small_in, 16)
            sp.dma_start(small[row_g:row_cb, :], g_norm.rearrange("(c p) -> c p", p=P)).then_inc(small_in, 16)
            sp.dma_start(small[row_cb:rows, :], b_conv.rearrange("(c p) -> c p", p=P)).then_inc(small_in, 16)
            sp.dma_start(gq[:, 0, :], g_q.rearrange("(a d) -> a d", a=1).to_broadcast([P, DH])).then_inc(g_in, 16)
            sp.dma_start(gq[:, 1, :], g_k.rearrange("(a d) -> a d", a=1).to_broadcast([P, DH])).then_inc(g_in, 16)
            for c in range(K):
                need(sp, wq_lo, c - 2)
                sp.dma_start(wq_raw[:, c % 3, :], wq_v[c]).then_inc(wq_in[c % 3], 16)
                need(sp, emb_mm, c - 1)
                sp.dma_start(emb_w[:, c % 2, :], emb_v[c]).then_inc(emb_in[c % 2], 16)
                if c:
                    store_wq(sp, c - 1)
            store_wq(sp, K - 1)
            for c in range(K):
                need(sp, wo_lo, c - 1)
                sp.dma_start(wo_raw[:, c % 2, :], wo_v[c]).then_inc(wo_in[c % 2], 16)
            sp.wait_ge(wq_out[0], 16 * (K // 2))
            sp.wait_ge(wq_out[1], 16 * (K // 2))

        @block.gpsimd
        def _(pool):
            nc.gpsimd.memset(const["eye32"][:], 0.0).then_inc(eye, 1)
            nc.gpsimd.memset(const["power"][:], -0.5)
            nc.gpsimd.memset(const["carry"][:], 1.0).then_inc(eye, 1)
            pool.wait_ge(eye, 2)
            nc.gpsimd.affine_select(out=const["eye32"][:], in_=const["eye32"][:], compare_op=ALU.not_equal,
                                    fill=1.0, base=0, pattern=[[-1, P]], channel_multiplier=1).then_inc(eye, 1)
            nc.gpsimd.memset(const["carry"][:].rearrange("p (b k) -> p b k", k=K)[:, :, 0:1], 0.0).then_inc(eye, 1)
            pool.wait_ge(eye, 4)
            nc.gpsimd.tensor_copy(const["eye16"][:], const["eye32"][:]).then_inc(eyed, 1)
            for c in range(K):
                pool.wait_ge(wq_hi, 3 * (c + 1))
                for j in range(3):
                    last = nc.gpsimd.tensor_tensor(by_head(c, 1, j), raw_by_head(c, j), by_head(c, 0, j),
                                                   ALU.subtract)
                last.then_inc(wq_lo, 1)
            for c in range(K):
                pool.wait_ge(wo_hi, c + 1)
                nc.gpsimd.tensor_tensor(const["wo"][:, c, 1, :], wo_raw[:, c % 2, :], const["wo"][:, c, 0, :],
                                        ALU.subtract).then_inc(wo_lo, 1)
            pool.wait_ge(top_in, 1)
            nc.gpsimd.partition_all_reduce(topr[:], top[:], P, RMAX).then_inc(top_all, 1)

        @block.scalar
        def _(act):
            for c in range(K):
                act.wait_ge(wq_scaled, c + 1)
                if c >= 2:
                    act.wait_ge(wq_out[c % 2], 16 * (c // 2))
                for j in range(3):
                    nc.scalar.activation(by_head(c, 0, j), raw_by_head(c, j), ACT.Copy).then_inc(wq_hi, 1)
            act.wait_ge(emb_mm, K)
            nc.scalar.activation(ss_row[:], ps_row[:], ACT.Copy).then_inc(emb_row, 1)
            for c in range(K):
                act.wait_ge(wo_scaled, c + 1)
                nc.scalar.activation(const["wo"][:, c, 0, :], wo_raw[:, c % 2, :], ACT.Copy).then_inc(wo_hi, 1)

        @block.tensor
        def _(pe):
            pe.wait_ge(small_in, 64)
            pe.wait_ge(eyed, 1)
            nc.tensor.transpose(ps_s[:, 0:rows], small[:], const["eye32"][0:rows, 0:rows]).then_inc(small_t, 1)
            pe.wait_ge(small_c, 1)
            cT = smallT[:, 0:B * K].rearrange("p (b c) -> p c b", c=K)
            for c in range(K):
                pe.wait_ge(emb_in[c % 2], 16 * (c // 2 + 1))
                for n in range(NE):
                    last = nc.tensor.matmul(ps_row[:, n * 512:(n + 1) * 512], cT[:, c, :],
                                            emb_w[:, c % 2, n * 512:(n + 1) * 512], start=(c == 0), stop=(c == K - 1))
                last.then_inc(emb_mm, 1)
            pe.wait_ge(emb_row, 1)
            for m in range(2 * K):
                last = nc.tensor.transpose(ps_t[:, m * B:(m + 1) * B], ss_row[:, m * P:(m + 1) * P],
                                           const["eye32"][0:B, 0:B])
            last.then_inc(emb_t, 1)

        @block.vector
        def _(v):
            steps = [0]

            def step(ins):
                steps[0] += 1
                ins.then_inc(dve, 1)
                v.wait_ge(dve, steps[0])

            def power_of_two(out, in_):
                step(nc.vector.tensor_scalar(in_, in_, TINY, None, ALU.max))
                step(nc.vector.tensor_scalar(out.bitcast(U32), in_.bitcast(U32), EXPONENT, None, ALU.bitwise_and))

            v.wait_ge(small_t, 1)
            nc.vector.tensor_copy(smallT[:], ps_s[:, 0:rows]).then_inc(small_c, 1)
            v.wait_ge(g_in, 32)
            step(nc.vector.tensor_tensor(const["g_qk"][:], gq[:, 0, :], gq[:, 1, :], ALU.mult))
            step(nc.vector.tensor_reduce(gmax[:, 0:1], const["g_qk"][:], axis=AX.X, op=ALU.max,
                                         apply_absolute_value=True))
            power_of_two(gmax[:, 1:2], gmax[:, 0:1])
            step(nc.vector.reciprocal(gmax[:, 2:3], gmax[:, 1:2]))
            step(nc.vector.tensor_scalar(const["g_qk"][:], const["g_qk"][:], gmax[:, 2:3], None, ALU.mult))
            step(nc.vector.tensor_scalar(const["l_scale"][:], gmax[:, 1:2], DH ** -0.5 / QK_UP ** 2, None, ALU.mult))
            for c in range(K):
                v.wait_ge(wq_in[c % 3], 16 * (c // 3 + 1))
                step(nc.vector.tensor_reduce(wq_max[:, c:c + 1], wq_raw[:, c % 3, :], axis=AX.X, op=ALU.max,
                                             apply_absolute_value=True))
                power_of_two(wq_two[:, c:c + 1], wq_max[:, c:c + 1])
                step(nc.vector.reciprocal(wq_inv[:, c:c + 1], wq_two[:, c:c + 1]))
                nc.vector.tensor_scalar(wq_raw[:, c % 3, :], wq_raw[:, c % 3, :], wq_inv[:, c:c + 1], W_UP,
                                        ALU.mult, ALU.mult).then_inc(wq_scaled, 1)
            for c in range(K):
                v.wait_ge(wo_in[c % 2], 16 * (c // 2 + 1))
                step(nc.vector.tensor_reduce(wo_max[:, c:c + 1], wo_raw[:, c % 2, :], axis=AX.X, op=ALU.max,
                                             apply_absolute_value=True))
                power_of_two(wo_two[:, c:c + 1], wo_max[:, c:c + 1])
                step(nc.vector.reciprocal(wo_inv[:, c:c + 1], wo_two[:, c:c + 1]))
                nc.vector.tensor_scalar(wo_raw[:, c % 2, :], wo_raw[:, c % 2, :], wo_inv[:, c:c + 1], W_UP,
                                        ALU.mult, ALU.mult).then_inc(wo_scaled, 1)
            v.wait_ge(emb_t, 1)
            step(nc.vector.tensor_tensor(
                ssT[:], ps_t[:, 0:2 * K * B].rearrange("p (m b) -> p m b", b=B),
                smallT[:, row_embb:row_g].rearrange("p (m a) -> p m a", a=1).to_broadcast([P, 2 * K, B]), ALU.add))
            step(nc.vector.tensor_scalar(mod[:, 0], ssT[:, 0:K, :], 1.0, None, ALU.add))
            step(nc.vector.tensor_tensor(
                mod[:, 0], mod[:, 0],
                smallT[:, row_g:row_cb].rearrange("p (m a) -> p m a", a=1).to_broadcast([P, K, B]), ALU.mult))
            step(nc.vector.tensor_copy(mod[:, 1], ssT[:, K:2 * K, :]))
            for i in range(2):
                step(nc.vector.tensor_tensor(
                    mod[:, i], mod[:, i], wq_two[:].rearrange("p (m a) -> p m a", a=1).to_broadcast([P, K, B]),
                    ALU.mult))
            for b in range(B):
                step(nc.vector.tensor_reduce(top[:, b:b + 1], mod[:, :, :, b], axis=AX.XY, op=ALU.max,
                                             apply_absolute_value=True))
            step(nc.vector.tensor_reduce(top[:, B:B + 1], wo_two[:], axis=AX.X, op=ALU.max))
            nc.vector.memset(gmax[:, 3:4], 0.0).then_inc(top_in, 1)
            v.wait_ge(top_all, 1)
            power_of_two(two[:], topr[:])
            step(nc.vector.reciprocal(twoi[:], two[:]))
            step(nc.vector.tensor_scalar(tmpb[:, 0], twoi[:, 0:B], X_UP, None, ALU.mult))
            for i, name in enumerate(("mod_a", "mod_s")):
                step(nc.vector.tensor_tensor(
                    wide[:, i], mod[:, i],
                    tmpb[:, 0].rearrange("p (a b) -> p a b", a=1).to_broadcast([P, K, B]), ALU.mult))
                for b in range(B):
                    step(nc.vector.tensor_copy(
                        const[name][:, b * K:(b + 1) * K, :],
                        wide[:, i, :, b].rearrange("p (a k) -> p a k", a=1).to_broadcast([P, K, K])))
            down = 1.0 / (X_UP * W_UP * QKV_DOWN)
            step(nc.vector.tensor_scalar(tmpb[:, 1], two[:, 0:B], down, None, ALU.mult))

            def by_unit(name):
                return const[name][:].rearrange("p (b k) -> p b k", k=K)

            def column(ap):
                return ap.rearrange("p (b a) -> p b a", a=1).to_broadcast([P, B, K])

            step(nc.vector.tensor_copy(by_unit("v_scale"), column(tmpb[:, 1])))
            step(nc.vector.tensor_tensor(tmpb[:, 2], twoi[:, 0:B], twoi[:, 0:B], ALU.mult))
            step(nc.vector.tensor_scalar(tmpb[:, 2], tmpb[:, 2], EPS / down ** 2 / QK_UP ** 2, None, ALU.mult))
            step(nc.vector.tensor_copy(by_unit("eps_u"), column(tmpb[:, 2])))
            step(nc.vector.tensor_scalar(const["o_row"][:], wo_two[:], twoi[:, B:B + 1], 0.5, ALU.mult, ALU.mult))
            step(nc.vector.tensor_scalar(tmpb[:, 1], tmpb[:, 1], two[:, B:B + 1], 2.0 / W_UP, ALU.mult, ALU.mult))
            step(nc.vector.tensor_copy(by_unit("y_scale"), column(tmpb[:, 1])))
            step(nc.vector.tensor_copy(const["taps"][:], smallT[:, 0:B * K].rearrange("p (b c) -> p b c", c=K)))
            step(nc.vector.tensor_scalar(const["taps"][:, B - 1, :], const["taps"][:, B - 1, :], 1.0, None, ALU.add))
            step(nc.vector.tensor_copy(const["conv_b"][:], smallT[:, row_cb:rows]))


def main(nc, const, w_dram, xn_dram, o_dram, x, W_qkv, out):
    B, N, D, K = dims(x, W_qkv)
    U = B * K
    NS = 2 * K
    KH = K // 2
    HC = K // 2
    HW = HC * P
    HN = N // 2
    LEAD = K + 2
    G = NS // 4
    TAPS = B
    H = TAPS - 1
    at = PLAN[K]
    x_t = x.rearrange("b n d -> (b n) d")
    out_t = out.rearrange("b n d -> (b n) d")
    with ExitStack() as ctx:
        def sb(name, shape, dt):
            return ctx.enter_context(nc.sbuf_tensor(name, shape, dt))

        def psum(name, shape, dt):
            return ctx.enter_context(nc.psum_tensor(name, shape, dt))

        def sem(name):
            return ctx.enter_context(nc.semaphore(name))

        w_sb = sb("w_sb", [P, 2, K, 2, 6 * DH], F16)
        xn_sb = sb("xn_sb", [P, 4, K, 2, P], F16)
        stage = sb("stage", [P, 2, 2 * KH, 3 * DH], F32)
        square = sb("square", [P, 4 * KH * DH], F32)
        q_pair = sb("q_pair", [P, 2 * KH, 2 * DH], F16)
        k_pair = sb("k_pair", [P, 2 * KH, 3 * DH], F16)
        stack = sb("stack", [P, 2, 2, 3, N], F16)
        v_pair = sb("v_pair", [P, 2, 2 * K, 2 * DH], F16)
        prob = sb("prob", [P, 4, N], F32)
        p_pair = sb("p_pair", [P, 4, 2, N], F16)
        pT = sb("pT", [P, 4, 2 * K, P], F16)
        o_lo = sb("o_lo", [P, 4, DH], F32)
        o_out = sb("o_out", [P, K, 2, DH], F32)
        y = sb("y", [P, D], F32)
        o_in = sb("o_in", [P, D], F32)
        half = sb("half", [P, 2, HC, P], F32)
        halfx = sb("halfx", [P, 2, HC, P], F32)
        oT = sb("oT", [P, K, 2, P], F16)
        yT = sb("yT", [P, K, H + P], F32)
        acc = sb("acc", [P, K, P], F32)
        fin = sb("fin", [P, D], F32)
        x_in = sb("x_in", [P, D], F32)
        xT = sb("xT", [P, K, 2, P], F16)
        neg = sb("neg", [P, NS], F32)
        bias = sb("bias", [P, NS], F32)
        total = sb("total", [P, 2 * NS], F32)
        inv = sb("inv", [P, 4], F32)
        ms = sb("ms", [P, 4 * KH], F32)
        rs = sb("rs", [P, 4 * KH], F32)
        msx = sb("msx", [P, 4], F32)

        scores = psum("scores", [P, 2, max(N, 1024)], F32)
        values = psum("values", [P, 2, 4, 2 * DH], F32)
        misc = psum("misc", [P, 2, 512], F32)

        gate = sem("gate")
        w_in = [sem(f"w_in{i}") for i in range(4)]
        xn_in = [sem(f"xn_in{i}") for i in range(4)]
        x_ld = sem("x_ld")
        x_sq = sem("x_sq")
        x_ms = sem("x_ms")
        x_pw = sem("x_pw")
        x_hat = sem("x_hat")
        x_tr = sem("x_tr")
        x_ev = sem("x_ev")
        x_hi = sem("x_hi")
        x_lo = sem("x_lo")
        x_mul = sem("x_mul")
        x_st = sem("x_st")
        qkv_mm = sem("qkv_mm")
        qkv_ev = sem("qkv_ev")
        h_sq = sem("h_sq")
        h_ss = sem("h_ss")
        h_ms = sem("h_ms")
        h_pw = sem("h_pw")
        h_n = sem("h_n")
        h_hi = sem("h_hi")
        h_lo = sem("h_lo")
        h_tr = sem("h_tr")
        h_ev = sem("h_ev")
        qk_done = sem("qk_done")
        max_done = sem("max_done")
        bias_done = sem("bias_done")
        exp_done = sem("exp_done")
        hi_done = sem("hi_done")
        lo_done = sem("lo_done")
        pT_in = [sem(f"pT_in{i}") for i in range(4)]
        pv_done = sem("pv_done")
        ov_copy = sem("ov_copy")
        ov_add = sem("ov_add")
        ov_inv = sem("ov_inv")
        ov_done = sem("ov_done")
        o_st = sem("o_st")
        o_ld = sem("o_ld")
        xo_ld = sem("xo_ld")
        last_o_ld = [sem(f"last_o_ld{i}") for i in range(2)]
        last_x_ld = [sem(f"last_x_ld{i}") for i in range(2)]
        o_tr = sem("o_tr")
        o_ev = sem("o_ev")
        o_hi = sem("o_hi")
        o_lo3 = sem("o_lo3")
        s_done = sem("s_done")
        op_mm = sem("op_mm")
        op_ev = sem("op_ev")
        y_tr = sem("y_tr")
        y_ev = sem("y_ev")
        halo = sem("halo")
        cv = sem("cv")
        f_tr = sem("f_tr")
        f_ev = sem("f_ev")
        f_st = sem("f_st")
        block = ctx.enter_context(nc.Block())

        stack_banks = ((0, 1, 0), (0, 1, 1))

        def in_units(eng, unit):
            last_x = U - LEAD

            def pairs(lo, hi, **parts):
                if lo < hi:
                    with eng.Fori(lo // 2, hi // 2) as j:
                        for parity in range(2):
                            unit(2 * j + parity, parity, **parts)

            unit(0, 0, qkv=True, xs=True, outs=False, fins=False)
            unit(1, 1, qkv=True, xs=True, outs=False, fins=False)
            pairs(2, K, qkv=True, xs=True, outs=False, fins=False)
            unit(K, 0, qkv=True, xs=K < last_x, outs=True, fins=False)
            unit(K + 1, 1, qkv=True, xs=K + 1 < last_x, outs=True, fins=True)
            pairs(K + 2, last_x, qkv=True, xs=True, outs=True, fins=True)
            pairs(max(last_x, K + 2), U - 2, qkv=True, xs=False, outs=True, fins=True)
            unit(U - 2, 0, qkv=True, xs=False, outs=True, fins=True)
            unit(U - 1, 1, qkv=False, xs=False, outs=True, fins=True)

        def in_last_tiles(eng, tile):
            tile(U - K, 0, first=True, last=False)
            tile(U - K + 1, 1, first=False, last=False)
            if K > 4:
                with eng.Fori((U - K) // 2 + 1, U // 2 - 1) as j:
                    for parity in range(2):
                        tile(2 * j + parity, parity, first=False, last=False)
            tile(U - 2, 0, first=False, last=False)
            tile(U - 1, 1, first=False, last=True)

        def half_bank(psum_banks, hh):
            return psum_banks[:, hh * 512:hh * 512 + HW]

        last_values = values[:].rearrange("p a s n -> p (a s n)")
        last_banks = dict(o=[half_bank(scores[:, 0], hh) for hh in range(2)],
                          y=[half_bank(scores[:, 1], hh) for hh in range(2)],
                          f=[half_bank(last_values, hh) for hh in range(2)])
        o_banks = [misc[:, 1, 0:HW], misc[:, 0, 0:HW]]
        x_banks = o_banks
        y_banks = o_banks
        f_banks = [misc[:, 0, 0:HW], misc[:, 1, 0:HW]]
        last_o_in = [prob[:, i, 0:D] for i in range(2)]
        last_y = [prob[:, 2 + i, 0:D] for i in range(2)]

        def last_loads(T, par):
            return 8 * (T - par - (U - K)) + 16

        def group(u, s):
            if isinstance(u, int) and NS * u + s < 8:
                return None
            return (G * u + s // 4 - 2, (s // 4) % 2)

        def four(u, s):
            return G * u + s // 4

        def slot(u, s):
            return NS * u + s

        @block.sync
        def _(sp):
            def passed():
                sp.sem_inc(gate, 1)

            def load_x(v):
                need(sp, x_tr, 2 * v)
                sp.dma_start(x_in[:], x_t[bass.ds(v * P, P), :]).then_inc(x_ld, 16)

            def store_xn(v):
                sp.wait_ge(x_hi, 2 * v + 2)
                sp.wait_ge(x_lo, 2 * v + 2)
                sp.dma_start(xn_dram[bass.ds(v, 1)].rearrange("a p n -> (a p) n"),
                             xT[:].rearrange("p c s n -> p (c s n)")).then_inc(x_st, 16)

            def load_w(w, par, i):
                need(sp, qkv_mm, K * (w - 1) + 1)
                cs = slice(i * K // 4, (i + 1) * K // 4)
                sp.dma_start(w_sb[:, par, cs].rearrange("p c s n -> p (c s n)"),
                             w_dram[bass.ds(w % K, 1), :, cs].rearrange("a p c s n -> (a p) (c s n)")
                             ).then_inc(w_in[i], 16)

            def load_xn(w, t):
                need(sp, qkv_mm, K * w + t - 3)
                need(sp, x_st, 16 * ((w // K) * K + t + 1))
                sp.dma_start(xn_sb[:, t % 4].rearrange("p c s n -> p (c s n)"),
                             xn_dram[bass.ds((w // K) * K + t, 1)].rearrange("a p n -> (a p) n")
                             ).then_inc(xn_in[t % 4], 16)

            def transpose_p(u, s):
                g = slot(u, s)
                sp.wait_ge(lo_done, g + 1)
                passed()
                need(sp, pv_done, g - 3)
                passed()
                sp.dma_start_transpose(pT[:, s % 4], p_pair[:, s % 4].rearrange("p a n -> p (a n)")
                                       ).then_inc(pT_in[s % 4], 16)

            def store_o(u):
                sp.wait_ge(ov_done, G * u + G)
                sp.dma_start(
                    o_dram[bass.ds((u // K) * K * P, K * P), bass.ds((u % K) * P, P)].rearrange(
                        "(t p) n -> p t n", p=P),
                    o_out[:].rearrange("p t h d -> p t (h d)")).then_inc(o_st, 16)

            def load_out(T):
                sp.wait_ge(o_st, 16 * ((T // K) * K + K))
                need(sp, o_tr, 2 * T)
                sp.dma_start(o_in[:], o_dram[bass.ds(T * P, P), :]).then_inc(o_ld, 16)

            def load_xo(T):
                need(sp, y_tr, 2 * T)
                sp.dma_start(y[:], x_t[bass.ds(T * P, P), :]).then_inc(xo_ld, 16)

            def store_out(T):
                sp.wait_ge(f_ev, 2 * T + 2)
                sp.dma_start(out_t[bass.ds(T * P, P), :], fin[:]).then_inc(f_st, 16)

            def unit(u, par, qkv, xs, outs, fins):
                w, v, T = u + 1, u + LEAD, u - K
                more = qkv and not (isinstance(u, int) and u + 2 >= U)
                for s in range(NS):
                    if xs and s == 0:
                        load_x(v)
                    g2 = s - 2
                    if g2 >= 0:
                        transpose_p(u, g2)
                    elif not (isinstance(u, int) and u == 0):
                        transpose_p(u - 1, NS + g2)
                    if qkv and 4 <= s + 3 < K and s >= 1:
                        load_xn(w, s + 3)
                    if more and K + 1 <= s < K + 5 and K == 8:
                        load_xn(w + 1, s - K - 1)
                    if more and K == 4 and s >= K:
                        load_xn(w + 1, s - K)
                    if more and s >= K and (s - K) % (K // 4) == 0:
                        load_w(w + 1, par, (s - K) // (K // 4))
                    if s == 5 % NS and not (isinstance(u, int) and u == 0):
                        store_o(u - 1)
                    if outs and s == at["ld"]:
                        load_xo(T)
                        load_out(T)
                    if fins and s == at["st"]:
                        store_out(T - 1)
                    if xs and s == at["xst"]:
                        store_xn(v)

            def load_last(T, par):
                need(sp, y_tr, 2 * T - 2)
                sp.dma_start(last_y[par], x_t[bass.ds(T * P, P), :]).then_inc(last_x_ld[par], 16)
                sp.wait_ge(o_tr, 2 * T - 2)
                sp.wait_ge(s_done, T - 1)
                sp.dma_start(last_o_in[par], o_dram[bass.ds(T * P, P), :]).then_inc(last_o_ld[par], 16)

            def last_tile(T, par, first, last):
                if not last:
                    load_last(T + 1, 1 - par)
                store_out(T - 1)

            for i in range(4):
                load_w(0, 0, i)
            for v in range(LEAD):
                load_x(v)
                if v:
                    store_xn(v - 1)
            store_xn(LEAD - 1)
            for t in range(K):
                load_xn(0, t)
            for i in range(4):
                load_w(1, 1, i)
            for t in range(4):
                load_xn(1, t)
            in_units(sp, unit)
            transpose_p(U - 1, NS - 2)
            transpose_p(U - 1, NS - 1)
            store_o(U - 1)
            sp.wait_ge(o_st, 16 * U)
            load_last(U - K, 0)
            in_last_tiles(sp, last_tile)
            store_out(U - 1)
            sp.wait_ge(f_st, 16 * U)

        @block.tensor
        def _(pe):
            def bank(i):
                return misc[:, i]

            def f16_bank(i):
                return misc[:, i].bitcast(F16).rearrange("p (a n) -> p a n", a=2)

            def qk(u, s, par):
                h, qt = s // K, s % K
                need(pe, exp_done, slot(u, s) - 1)
                for n in range(2):
                    for i in range(2):
                        last = nc.tensor.matmul(scores[:, s % 2, n * HN:(n + 1) * HN],
                                                stack[:, par, h, 0, qt * P:(qt + 1) * P],
                                                stack[:, par, h, 1 + i, n * HN:(n + 1) * HN],
                                                start=(i == 0), stop=(i == 1))
                last.then_inc(qk_done, 1)

            def pv(u, s, par):
                h = s // K
                g = slot(u, s)
                if s % 4 == 0:
                    need(pe, ov_done, four(u, s) - 1)
                pe.wait_ge(pT_in[s % 4], 16 * (four(u, s) + 1))
                o = values[:, (s // 4) % 2, s % 4, :]
                for t in range(K - 1):
                    nc.tensor.matmul(o, pT[:, s % 4, t, :], v_pair[:, par, 2 * t + h, :],
                                     start=(t == 0), stop=False)
                for t in range(K):
                    nc.tensor.matmul(o[:, 0:DH], pT[:, s % 4, K + t, :], v_pair[:, par, 2 * t + h, 0:DH],
                                     start=False, stop=False)
                last = nc.tensor.matmul(o, pT[:, s % 4, K - 1, :], v_pair[:, par, 2 * (K - 1) + h, :],
                                        start=False, stop=True)
                last.then_inc(pv_done, 1)

            def project(w, par, t, before=None):
                if t >= 2:
                    pe.wait_ge(qkv_ev, K * w + t - 1)
                if before:
                    pe.wait_ge(*before)
                pe.wait_ge(xn_in[t % 4], 16 * (K // 4 * w + t // 4 + 1))
                acc_ = bank(t % 2)[:, 0:6 * DH]
                for c in range(K):
                    if t == 0 and c % (K // 4) == 0:
                        pe.wait_ge(w_in[c // (K // 4)], 16 * (w + 1))
                    for i, j in ((0, 0), (0, 1), (1, 0)):
                        last = nc.tensor.matmul(acc_, xn_sb[:, t % 4, c, i, :], w_sb[:, par, c, j, :],
                                                start=(c == 0 and i == j == 0), stop=(c == K - 1 and i == 1))
                last.then_inc(qkv_mm, 1)

            def stacks(w, hf, i, before):
                pe.wait_ge(h_lo, 3 * (2 * w + hf) + 2)
                pe.wait_ge(h_hi, 3 * (2 * w + hf) + 2)
                need(pe, *before)
                b = stack_banks[hf][i]
                for t in range(KH):
                    for a in range(2):
                        src = ((q_pair[:, 2 * t + i, :] if a == 0 else k_pair[:, 2 * t + i, 0:2 * DH])
                               if i < 2 else k_pair[:, 2 * t + a, DH:3 * DH])
                        last = nc.tensor.transpose(f16_bank(b)[:, a, t * P:(t + 1) * P], src, const["eye16"][:])
                last.then_inc(h_tr, 1)

            def transposes(dst, src, done):
                for c in range(HC):
                    last = nc.tensor.transpose(dst[:, c * P:(c + 1) * P], src(c), const["eye32"][:])
                last.then_inc(done, 1)

            def x_transposes(v, hh, before):
                pe.wait_ge(x_hat, v + 1)
                need(pe, *before)
                transposes(x_banks[hh], lambda c: x_in[:, (hh * HC + c) * P:(hh * HC + c + 1) * P], x_tr)

            def o_transposes(T, hh, banks, src, loaded, before):
                pe.wait_ge(*loaded)
                need(pe, *before)
                transposes(banks[hh], lambda c: src[:, (hh * HC + c) * P:(hh * HC + c + 1) * P], o_tr)

            def out_product(T, n, part, before=None):
                pe.wait_ge(o_hi, 2 * T + part + 1)
                pe.wait_ge(o_lo3, 2 * T + part + 1)
                if before:
                    pe.wait_ge(*before)
                for c in range(part * HC, (part + 1) * HC):
                    for i, j in ((0, 0), (0, 1), (1, 0)):
                        last = nc.tensor.matmul(bank(1 - n)[:, 0:HN], oT[:, c, i, :],
                                                const["wo"][:, c, j, n * HN:(n + 1) * HN],
                                                start=(c == 0 and i == j == 0), stop=(c == K - 1 and i == 1))
                if part == 1:
                    last.then_inc(op_mm, 1)

            def y_transposes(T, hh, banks, src, before):
                pe.wait_ge(op_ev, 2 * T + hh + 1)
                need(pe, *before)
                transposes(banks[hh], lambda c: src[:, (hh * HC + c) * P:(hh * HC + c + 1) * P], y_tr)

            def out_transposes(T, hh, banks, before):
                pe.wait_ge(cv, TAPS * K * T + TAPS * HC * (hh + 1))
                need(pe, *before)
                transposes(banks[hh], lambda c: acc[:, hh * HC + c, :], f_tr)

            def unit(u, par, qkv, xs, outs, fins):
                w, v, T = u + 1, u + LEAD, u - K
                for s in range(NS):
                    if s == 0:
                        pe.wait_ge(h_ev, 6 * (u + 1))
                    qk(u, s, par)
                    if fins and s == at["fin"]:
                        out_transposes(T - 1, 0, f_banks, (qkv_ev, K * w + KH - 1) if qkv else (y_ev, 2 * T))
                    if qkv and s == at["h01"]:
                        stacks(w, 0, 1, (qkv_ev, K * w + K))
                    if outs and s == at["ot"]:
                        o_transposes(T, 0, o_banks, o_in, (o_ld, 16 * (T + 1)),
                                     (h_ev, 6 * w + 2) if qkv else (f_ev, 2 * T))
                    if xs and s == at["xt"]:
                        x_transposes(v, 0, (o_ev, 2 * T + 1) if outs else (h_ev, 6 * w + 2))
                    if outs and s == at["op0a"]:
                        out_product(T, 0, 0, (x_ev, 2 * v + 1) if xs else (o_ev, 2 * T + 1))
                    if outs and s == at["op1b"] != at["op1a"]:
                        out_product(T, 1, 1)
                    if outs and s == at["yt"] != at["op1b"]:
                        y_transposes(T, 0, y_banks, y, (h_ev, 6 * w + 6) if qkv else (op_ev, 2 * T + 1))
                    if s >= LAG:
                        pv(u, s - LAG, par)
                    elif not (isinstance(u, int) and u == 0):
                        pv(u - 1, NS + s - LAG, 1 - par)
                    if fins and s == at["fin"]:
                        out_transposes(T - 1, 1, f_banks, (qkv_ev, K * w + KH) if qkv else (y_ev, 2 * T))
                    if qkv and s < K:
                        before = None
                        if fins and s < 2:
                            before = (y_ev, 2 * T)
                        if fins and KH <= s < KH + 2:
                            before = (f_ev, 2 * T - 1 + s - KH)
                        project(w, 1 - par, s, before)
                    if qkv and s == at["h00"]:
                        stacks(w, 0, 0, (qkv_ev, K * w + K - 1))
                    if qkv and s == at["h02"]:
                        stacks(w, 0, 2, (h_ev, 6 * w + 1))
                    if outs and s == at["ot"]:
                        o_transposes(T, 1, o_banks, o_in, (o_ld, 16 * (T + 1)),
                                     (h_ev, 6 * w + 3) if qkv else (f_ev, 2 * T))
                    if xs and s == at["xt"]:
                        x_transposes(v, 1, (o_ev, 2 * T + 2) if outs else (h_ev, 6 * w + 3))
                    if outs and s == at["op0b"]:
                        out_product(T, 0, 1)
                    if qkv and s == at["h10"]:
                        stacks(w, 1, 0, (x_ev, 2 * v + 2) if xs else (o_ev, 2 * T + 2))
                    if outs and s == at["op1a"]:
                        out_product(T, 1, 0, (h_ev, 6 * w + 4) if qkv else (o_ev, 2 * T + 2))
                    if qkv and s == at["h11"]:
                        stacks(w, 1, 1, (op_ev, 2 * T + 1) if outs else (x_ev, 2 * v + 1))
                    if outs and s == at["op1b"] == at["op1a"]:
                        out_product(T, 1, 1)
                    if qkv and s == at["h12"]:
                        stacks(w, 1, 2, (h_ev, 6 * w + 5))
                    if outs and s == at["yt"]:
                        if at["yt"] == at["op1b"]:
                            y_transposes(T, 0, y_banks, y, (h_ev, 6 * w + 6) if qkv else (op_ev, 2 * T + 1))
                        y_transposes(T, 1, y_banks, y, (op_ev, 2 * T + 2))

            def last_o_transposes(T, par, before):
                for hh in range(2):
                    o_transposes(T, hh, last_banks["o"], last_o_in[par], (last_o_ld[par], last_loads(T, par)),
                                 (o_ev, 2 * T - 1 + hh) if before is None else before)

            def last_tile(T, par, first, last):
                out_product(T, 0, 0, (y_ev, 2 * T) if first else (op_ev, 2 * T - 1))
                out_product(T, 0, 1)
                if not first:
                    y_transposes(T - 1, 1, last_banks["y"], last_y[1 - par], (y_ev, 2 * T - 2))
                if not last:
                    last_o_transposes(T + 1, 1 - par, None)
                out_product(T, 1, 0, (y_ev, 2 * T) if first else (op_ev, 2 * T))
                out_product(T, 1, 1)
                y_transposes(T, 0, last_banks["y"], last_y[par], (exp_done, NS * U) if first else (y_ev, 2 * T - 1))
                for hh in range(2):
                    out_transposes(T - 1, hh, last_banks["f"],
                                   (ov_done, G * U) if first else (f_ev, 2 * T - 3 + hh))

            for v in range(LEAD):
                for hh in range(2):
                    x_transposes(v, hh, (x_ev, 2 * v - 1 + hh))
            pe.wait_ge(x_ev, 2 * LEAD)
            for t in range(K):
                project(0, 0, t)
            for hf, before in enumerate((((qkv_ev, K - 1), (qkv_ev, K), (h_ev, 1)),
                                         ((h_ev, 3), (h_ev, 2), (h_ev, 5)))):
                for i in range(3):
                    stacks(0, hf, i, before[i])
            in_units(pe, unit)
            for s in range(NS - LAG, NS):
                pv(U - 1, s, 1)
            last_o_transposes(U - K, 0, (exp_done, NS * U))
            in_last_tiles(pe, last_tile)
            y_transposes(U - 1, 1, last_banks["y"], last_y[1], (y_ev, 2 * U - 2))
            for hh in range(2):
                out_transposes(U - 1, hh, last_banks["f"], (f_ev, 2 * U - 3 + hh))

        @block.scalar
        def _(act):
            def exponent(u, s, par):
                g = slot(u, s)
                act.wait_ge(bias_done, g + 1)
                need(act, lo_done, g - 3)
                if s % 4 == 0:
                    need(act, ov_inv, four(u, s) - 7)
                nc.scalar.activation(prob[:, s % 4, :], scores[:, s % 2, 0:N], ACT.Exp, bias=bias[:, s:s + 1],
                                     scale=const["l_scale"][:, 0:1],
                                     accum_out=total[:, par * NS + s:par * NS + s + 1]).then_inc(exp_done, 1)

            def read_projection(w, t):
                hf = t // KH
                act.wait_ge(qkv_mm, K * w + t + 1)
                if t % KH == 0:
                    need(act, h_lo, 3 * (2 * (w - 1) + hf + 1))
                nc.scalar.activation(stage[:, hf, 2 * (t % KH):2 * (t % KH) + 2, :],
                                     misc[:, t % 2, 0:6 * DH].rearrange("p (h n) -> p h n", h=2), ACT.Copy,
                                     scale=QKV_DOWN).then_inc(qkv_ev, 1)

            def squares(w, hf):
                act.wait_ge(qkv_ev, K * w + (hf + 1) * KH)
                need(act, h_ss, 2 * w + hf)
                nc.scalar.activation(square[:].rearrange("p (t n) -> p t n", n=2 * DH),
                                     stage[:, hf, :, 0:2 * DH], ACT.Square).then_inc(h_sq, 1)

            def high_halves(w, par, hf):
                act.wait_ge(h_n, 2 * (2 * w + hf) + 2)
                need(act, h_tr, 3 * (2 * w + hf))
                nc.scalar.activation(q_pair[:, :, 0:DH], stage[:, hf, :, 0:DH], ACT.Copy).then_inc(h_hi, 1)
                kk = k_pair[:].rearrange("p t (a d) -> p t a d", d=DH)
                for a in (0, 2):
                    last = nc.scalar.activation(kk[:, :, a, :], stage[:, hf, :, DH:2 * DH], ACT.Copy)
                last.then_inc(h_hi, 1)
                need(act, pv_done, NS * (w - 1))
                nc.scalar.activation(v_pair[:, par, 2 * KH * hf:2 * KH * (hf + 1), 0:DH],
                                     stage[:, hf, :, 2 * DH:3 * DH], ACT.Copy).then_inc(h_hi, 1)

            def read_stacks(w, par, hf, i):
                act.wait_ge(h_tr, 3 * (2 * w + hf) + i + 1)
                dst = stack[:, par, i, 0:2, hf * HN:(hf + 1) * HN] if i < 2 else \
                    stack[:, par, :, 2, hf * HN:(hf + 1) * HN]
                b = stack_banks[hf][i]
                nc.scalar.activation(dst, misc[:, b].bitcast(F16).rearrange("p (a n) -> p a n", a=2)[:, :, 0:HN],
                                     ACT.Copy).then_inc(h_ev, 1)

            def x_square(v, ss_count):
                act.wait_ge(x_ld, 16 * (v + 1))
                need(act, h_ss, ss_count)
                need(act, x_ms, v)
                nc.scalar.activation(square[:, 0:D].bitcast(F16)[:, 0:D], x_in[:], ACT.Square,
                                     accum_out=msx[:, 0:1]).then_inc(x_sq, 1)

            def x_scale(v):
                act.wait_ge(x_pw, v + 1)
                nc.scalar.activation(x_in[:], x_in[:], ACT.Copy, scale=msx[:, 2:3]).then_inc(x_hat, 1)

            def x_high(v):
                for hh in range(2):
                    act.wait_ge(x_ev, 2 * v + hh + 1)
                    need(act, x_st, 16 * v)
                    nc.scalar.activation(xT[:, hh * HC:(hh + 1) * HC, 0, :], halfx[:, hh], ACT.Copy).then_inc(x_hi, 1)

            def read_values_low(q):
                count, b = q
                act.wait_ge(pv_done, 4 * count + 4)
                need(act, ov_done, count)
                nc.scalar.activation(o_lo[:], values[:, b, :, DH:2 * DH], ACT.Copy).then_inc(ov_copy, 1)

            def o_high(T):
                for hh in range(2):
                    act.wait_ge(o_ev, 2 * T + hh + 1)
                    need(act, op_mm, 2 * T)
                    nc.scalar.activation(oT[:, hh * HC:(hh + 1) * HC, 0, :], half[:, hh], ACT.Copy).then_inc(o_hi, 1)

            def read_yT(T, hh, banks):
                act.wait_ge(y_tr, 2 * T + hh + 1)
                act.wait_ge(halo, T + 1)
                nc.scalar.activation(yT[:, hh * HC:(hh + 1) * HC, H:H + P],
                                     banks[hh].rearrange("p (c n) -> p c n", n=P), ACT.Copy).then_inc(y_ev, 1)

            def read_out(T, hh, banks):
                act.wait_ge(f_tr, 2 * T + hh + 1)
                need(act, f_st, 16 * T)
                nc.scalar.activation(fin[:, hh * HW:(hh + 1) * HW], banks[hh], ACT.Copy).then_inc(f_ev, 1)

            def unit(u, par, qkv, xs, outs, fins):
                w, v, T = u + 1, u + LEAD, u - K
                for s in range(NS):
                    if fins and s == 0:
                        read_yT(T - 1, 1, y_banks)
                    if fins and s == at["fin"]:
                        read_out(T - 1, 0, f_banks)
                    for name, hf, i in (("h00", 0, 0), ("h10", 1, 0), ("h11", 1, 1), ("h12", 1, 2)):
                        if qkv and s == at[name] + 1 < NS:
                            read_stacks(w, 1 - par, hf, i)
                    if qkv and s == at["h01"]:
                        read_stacks(w, 1 - par, 0, 1)
                    exponent(u, s, par)
                    if s % 4 == 0:
                        q = group(u, s)
                        if q:
                            read_values_low(q)
                    if fins and s == at["fin"]:
                        read_out(T - 1, 1, f_banks)
                    if qkv and s < K:
                        read_projection(w, s)
                    if qkv and s == at["h02"]:
                        read_stacks(w, 1 - par, 0, 2)
                    if outs and s == at["ohi"]:
                        o_high(T)
                    if xs and s == at["xhi"]:
                        x_high(v)
                    if xs and s == at["xs"]:
                        x_square(v, 2 * w)
                    if xs and s == at["xh"]:
                        x_scale(v)
                    for hf in range(2):
                        if qkv and s == at[f"sq{hf}"]:
                            squares(w, hf)
                        if qkv and s == at[f"hi{hf}"]:
                            high_halves(w, 1 - par, hf)
                    for name, hf, i in (("h11", 1, 1), ("h12", 1, 2)):
                        if qkv and s == at[name] == NS - 1:
                            read_stacks(w, 1 - par, hf, i)
                    if outs and s == at["yt"]:
                        read_yT(T, 0, y_banks)

            def last_tile(T, par, first, last):
                if first:
                    read_yT(T - 1, 1, y_banks)
                else:
                    read_yT(T - 1, 1, last_banks["y"])
                if not last:
                    o_high(T + 1)
                read_yT(T, 0, last_banks["y"])
                for hh in range(2):
                    read_out(T - 1, hh, last_banks["f"])

            for v in range(LEAD):
                x_square(v, 0)
                x_scale(v)
                x_high(v)
            for hf in range(2):
                for t in range(KH * hf, KH * (hf + 1)):
                    read_projection(0, t)
                squares(0, hf)
            for hf in range(2):
                high_halves(0, 0, hf)
                for i in range(3):
                    read_stacks(0, 0, hf, i)
            in_units(act, unit)
            for i in range(2):
                read_values_low((G * U - 2 + i, i))
            o_high(U - K)
            in_last_tiles(act, last_tile)
            read_yT(U - 1, 1, last_banks["y"])
            for hh in range(2):
                read_out(U - 1, hh, last_banks["f"])

        @block.gpsimd
        def _(pool):
            def low(u, s):
                pool.wait_ge(hi_done, slot(u, s) + 1)
                nc.gpsimd.tensor_tensor(p_pair[:, s % 4, 1, :], prob[:, s % 4, :], p_pair[:, s % 4, 0, :],
                                        ALU.subtract).then_inc(lo_done, 1)

            def half_power(w, hf):
                pool.wait_ge(h_ms, 2 * w + hf + 1)
                need(pool, h_n, 2 * (2 * w + hf))
                nc.gpsimd.tensor_tensor(rs[:], ms[:], const["power"][:, 0:4 * KH], ALU.pow).then_inc(h_pw, 1)

            def half_low(w, par, hf):
                n = 2 * w + hf
                pool.wait_ge(h_hi, 3 * n + 3)
                nc.gpsimd.tensor_tensor(q_pair[:, :, DH:2 * DH], stage[:, hf, :, 0:DH], q_pair[:, :, 0:DH],
                                        ALU.subtract).then_inc(h_lo, 1)
                nc.gpsimd.tensor_tensor(k_pair[:, :, DH:2 * DH], stage[:, hf, :, DH:2 * DH], k_pair[:, :, 0:DH],
                                        ALU.subtract).then_inc(h_lo, 1)
                vp = v_pair[:, par, 2 * KH * hf:2 * KH * (hf + 1), :]
                nc.gpsimd.tensor_tensor(vp[:, :, DH:2 * DH], stage[:, hf, :, 2 * DH:3 * DH], vp[:, :, 0:DH],
                                        ALU.subtract).then_inc(h_lo, 1)

            def x_power(v):
                pool.wait_ge(x_ms, v + 1)
                need(pool, x_hat, v)
                nc.gpsimd.tensor_tensor(msx[:, 2:3], msx[:, 1:2], const["power"][:, 0:1], ALU.pow).then_inc(x_pw, 1)

            def x_low(v):
                for hh in range(2):
                    pool.wait_ge(x_hi, 2 * v + hh + 1)
                    nc.gpsimd.tensor_tensor(xT[:, hh * HC:(hh + 1) * HC, 1, :], halfx[:, hh],
                                            xT[:, hh * HC:(hh + 1) * HC, 0, :], ALU.subtract).then_inc(x_lo, 1)

            def o_low(T):
                for hh in range(2):
                    pool.wait_ge(o_hi, 2 * T + hh + 1)
                    nc.gpsimd.tensor_tensor(oT[:, hh * HC:(hh + 1) * HC, 1, :], half[:, hh],
                                            oT[:, hh * HC:(hh + 1) * HC, 0, :], ALU.subtract).then_inc(o_lo3, 1)

            def unit(u, par, qkv, xs, outs, fins):
                w, v, T = u + 1, u + LEAD, u - K
                for s in range(NS):
                    if s:
                        low(u, s - 1)
                    elif not (isinstance(u, int) and u == 0):
                        low(u - 1, NS - 1)
                    if outs and s == at["olo"]:
                        o_low(T)
                    if xs and s == at["xlo"]:
                        x_low(v)
                    if xs and s == at["xs"]:
                        x_power(v)
                    for hf in range(2):
                        if qkv and s == at[f"ss{hf}"]:
                            half_power(w, hf)
                        if qkv and s == at[f"lo{hf}"]:
                            half_low(w, 1 - par, hf)

            for v in range(LEAD):
                x_power(v)
                x_low(v)
            for hf in range(2):
                half_power(0, hf)
                half_low(0, 0, hf)
            in_units(pool, unit)
            low(U - 1, NS - 1)
            o_low(U - K)
            in_last_tiles(pool, lambda T, par, first, last: None if last else o_low(T + 1))

        @block.vector
        def _(dve):
            def maximum(u, s):
                g = slot(u, s)
                dve.wait_ge(qk_done, g + 1)
                nc.vector.tensor_reduce(neg[:, s:s + 1], scores[:, s % 2, 0:N], axis=AX.X, op=ALU.max,
                                        negate=True).then_inc(max_done, 1)
                dve.wait_ge(max_done, g + 1)
                nc.vector.tensor_scalar(bias[:, s:s + 1], neg[:, s:s + 1], const["l_scale"][:, 0:1], P_SHIFT,
                                        ALU.mult, ALU.add).then_inc(bias_done, 1)

            def high(u, s):
                g = slot(u, s)
                dve.wait_ge(exp_done, g + 1)
                need(dve, pT_in[s % 4], 16 * four(u, s))
                nc.vector.tensor_copy(p_pair[:, s % 4, 0, :], prob[:, s % 4, :]).then_inc(hi_done, 1)

            def sums(w, hf):
                n = 2 * w + hf
                dve.wait_ge(h_sq, n + 1)
                nc.vector.tensor_reduce(ms[:], square[:].rearrange("p (t d) -> p t d", d=DH), axis=AX.X,
                                        op=ALU.add).then_inc(h_ss, 1)
                dve.wait_ge(h_ss, n + 1)
                nc.vector.tensor_scalar(ms[:], ms[:], 1.0 / (DH * QK_UP ** 2), const["eps_u"][:, bass.ds(w, 1)],
                                        ALU.mult, ALU.add).then_inc(h_ms, 1)

            def normalise(w, hf):
                n = 2 * w + hf
                dve.wait_ge(h_pw, n + 1)
                qk_ = stage[:, hf, :, 0:2 * DH].rearrange("p t (j d) -> p t j d", d=DH)
                r_ = rs[:].rearrange("p (t j a) -> p t j a", j=2, a=1).to_broadcast([P, 2 * KH, 2, DH])
                nc.vector.tensor_tensor(qk_, qk_, r_, ALU.mult).then_inc(h_n, 1)
                dve.wait_ge(h_n, 2 * n + 1)
                q_ = stage[:, hf, :, 0:DH]
                g_ = const["g_qk"][:].rearrange("p (a d) -> p a d", a=1).to_broadcast([P, 2 * KH, DH])
                nc.vector.tensor_tensor(q_, q_, g_, ALU.mult).then_inc(h_n, 1)

            def x_mean(v):
                dve.wait_ge(x_sq, v + 1)
                need(dve, x_pw, v)
                nc.vector.tensor_scalar(msx[:, 1:2], msx[:, 0:1], 1.0 / D, EPS, ALU.mult, ALU.add).then_inc(x_ms, 1)

            def x_modulate(v):
                for hh in range(2):
                    dve.wait_ge(x_tr, 2 * v + hh + 1)
                    need(dve, x_lo, 2 * v - 1 + hh)

                    def mod(name):
                        m = const[name][:, bass.ds(v, 1), hh * HC:(hh + 1) * HC]
                        return m.rearrange("p a (c b) -> p (a c) b", b=1).to_broadcast([P, HC, P])

                    nc.vector.tensor_tensor(halfx[:, hh], x_banks[hh].rearrange("p (c n) -> p c n", n=P),
                                            mod("mod_a"), ALU.mult).then_inc(x_mul, 1)
                    dve.wait_ge(x_mul, 2 * v + hh + 1)
                    nc.vector.tensor_tensor(halfx[:, hh], halfx[:, hh], mod("mod_s"), ALU.add).then_inc(x_ev, 1)

            def read_values(q, tile, head, col):
                count, b = q
                dve.wait_ge(exp_done, 4 * count + 4)
                nc.vector.reciprocal(inv[:], total[:, col:col + 4]).then_inc(ov_inv, 1)
                dve.wait_ge(ov_copy, count + 1)
                nc.vector.tensor_tensor(o_lo[:], values[:, b, :, 0:DH], o_lo[:], ALU.add).then_inc(ov_add, 1)
                dve.wait_ge(ov_add, count + 1)
                nc.vector.tensor_tensor(
                    o_out[:, tile:tile + 4, head, :], o_lo[:],
                    inv[:].rearrange("p (t a) -> p t a", a=1).to_broadcast([P, 4, DH]), ALU.mult).then_inc(ov_done, 1)

            def values_at(u, s, par):
                q = group(u, s)
                if not q:
                    return
                first = (s - 8) % NS
                upar = par if s >= 8 else 1 - par
                if first == 0:
                    need(dve, o_st, 16 * (u if s >= 8 else u - 1))
                dve_read(q, first, upar)

            def dve_read(q, first, upar):
                need(dve, ov_done, q[0])
                read_values(q, first % K, first // K, upar * NS + first)

            def residual(T, o_, y_, loaded):
                for wait in loaded:
                    dve.wait_ge(*wait)
                nc.vector.scalar_tensor_tensor(out=y_, in0=o_, scalar=const["v_scale"][:, bass.ds(T, 1)],
                                               in1=y_, op0=ALU.mult, op1=ALU.add).then_inc(s_done, 1)

            def o_scale(T, hh, banks):
                dve.wait_ge(o_tr, 2 * T + hh + 1)
                need(dve, o_lo3, 2 * T - 1 + hh)
                m = const["o_row"][:, hh * HC:(hh + 1) * HC].rearrange("p (c b) -> p c b", b=1)
                nc.vector.tensor_tensor(half[:, hh], banks[hh].rearrange("p (c n) -> p c n", n=P),
                                        m.to_broadcast([P, HC, P]), ALU.mult).then_inc(o_ev, 1)

            def add_product(T, n, y_):
                dve.wait_ge(op_mm, 2 * T + n + 1)
                dve.wait_ge(s_done, T + 1)
                ys = y_[:, n * HN:(n + 1) * HN]
                nc.vector.scalar_tensor_tensor(out=ys, in0=misc[:, 1 - n, 0:HN],
                                               scalar=const["y_scale"][:, bass.ds(T, 1)],
                                               in1=ys, op0=ALU.mult, op1=ALU.add).then_inc(op_ev, 1)

            def carry_tokens(T):
                need(dve, cv, TAPS * K * T)
                nc.vector.tensor_scalar(yT[:, :, 0:H], yT[:, :, P:P + H], const["carry"][:, bass.ds(T, 1)], None,
                                        ALU.mult).then_inc(halo, 1)

            def convolve(T, quarter):
                chunks = K // 4
                dve.wait_ge(y_ev, 2 * T + quarter // 2 + 1)
                need(dve, f_tr, 2 * T)
                base = TAPS * K * T + TAPS * chunks * quarter
                for k in range(TAPS - 1, -1, -1):
                    for i in range(chunks):
                        c = quarter * chunks + i
                        if k == TAPS - 1:
                            nc.vector.tensor_scalar(acc[:, c, :], yT[:, c, k:k + P], const["taps"][:, k, c:c + 1],
                                                    const["conv_b"][:, c:c + 1], ALU.mult, ALU.add).then_inc(cv, 1)
                        else:
                            dve.wait_ge(cv, base + chunks * (TAPS - 2 - k) + i + 1)
                            nc.vector.scalar_tensor_tensor(out=acc[:, c, :], in0=yT[:, c, k:k + P],
                                                           scalar=const["taps"][:, k, c:c + 1], in1=acc[:, c, :],
                                                           op0=ALU.mult, op1=ALU.add).then_inc(cv, 1)

            def unit(u, par, qkv, xs, outs, fins):
                w, v, T = u + 1, u + LEAD, u - K
                for s in range(NS):
                    if outs and s == at["yt"] != at["op1b"]:
                        add_product(T, 1, y)
                    maximum(u, s)
                    if outs and s == at["op0b"] + 1:
                        add_product(T, 0, y)
                        carry_tokens(T)
                    if outs and s == at["ot"]:
                        o_scale(T, 0, o_banks)
                    if s:
                        high(u, s - 1)
                    elif not (isinstance(u, int) and u == 0):
                        high(u - 1, NS - 1)
                    if s % 4 == 0:
                        values_at(u, s, par)
                    if outs and s == at["res"]:
                        residual(T, o_in[:], y[:], ((xo_ld, 16 * (T + 1)), (o_ld, 16 * (T + 1))))
                    if outs and s == at["ot"]:
                        o_scale(T, 1, o_banks)
                    if xs and s == at["xt"]:
                        x_modulate(v)
                    if xs and s == at["xs"]:
                        x_mean(v)
                    for hf in range(2):
                        if qkv and s == at[f"ss{hf}"]:
                            sums(w, hf)
                        if qkv and s == at[f"n{hf}"]:
                            normalise(w, hf)
                    if outs and s == at["yt"] == at["op1b"]:
                        add_product(T, 1, y)
                    for quarter in range(4):
                        if fins and s == at["cv"][quarter]:
                            convolve(T - 1, quarter)

            def last_head(T, par):
                residual(T, last_o_in[par], last_y[par],
                         ((last_x_ld[par], last_loads(T, par)), (last_o_ld[par], last_loads(T, par))))
                for hh in range(2):
                    o_scale(T, hh, last_banks["o"])

            def last_tile(T, par, first, last):
                if not last:
                    last_head(T + 1, 1 - par)
                add_product(T, 0, last_y[par])
                for quarter in range(4):
                    convolve(T - 1, quarter)
                carry_tokens(T)
                add_product(T, 1, last_y[par])

            nc.vector.memset(yT[:], 0.0)
            for v in range(LEAD):
                x_mean(v)
                x_modulate(v)
            for hf in range(2):
                sums(0, hf)
                normalise(0, hf)
            in_units(dve, unit)
            high(U - 1, NS - 1)
            for i in range(2):
                dve_read((G * U - 2 + i, i), NS - 8 + 4 * i, 1)
            last_head(U - K, 0)
            in_last_tiles(dve, last_tile)
            for quarter in range(4):
                convolve(U - 1, quarter)


_INS = ["x", "cond_2048", "L0_cond_W_emb", "L0_cond_b_emb", "L0_cond_g_norm", "L0_cond_W_qkv",
        "L0_cond_g_q", "L0_cond_g_k", "L0_cond_W_out", "L1_cond_b"]


def kernel(**inputs):
    import numpy as _np
    import concourse.bacc as _bacc
    from concourse import mybir as _mybir
    from concourse.bass_utils import run_bass_kernel_spmd as _run

    nc = _bacc.Bacc("TRN2", target_bir_lowering=False, num_devices=1, dynamic_dma_scratch_size=1024)
    arrays, args = {}, []
    for name in _INS:
        a = _np.ascontiguousarray(inputs[name])
        arrays[f"in_{name}"] = a
        args.append(nc.dram_tensor(f"in_{name}", a.shape, _mybir.dt.from_np(a.dtype), kind="ExternalInput").ap())
    args.append(nc.dram_tensor("out_0", inputs["x"].shape, _mybir.dt.float32, kind="ExternalOutput").ap())
    bass_cond_attention_conv(nc, *args)
    r = _run(nc, [arrays], core_ids=[0])
    return r.results[0]["out_0"]
```

```python
from contextlib import ExitStack

import numpy as np

import concourse.bass as bass
from concourse import mybir

P = 128
F32 = mybir.dt.float32
F16 = mybir.dt.float16
U32 = mybir.dt.uint32
I32 = mybir.dt.int32
ALU = mybir.AluOpType
ACT = mybir.ActivationFunctionType
AX = mybir.AxisListType
RMAX = bass.bass_isa.ReduceOp.max

EPS = 1e-6
DH = 64
LAG = 4
X_UP = 256.0
W_UP = 1024.0
QKV_DOWN = 2.0 ** -16
QK_UP = 64.0
P_SHIFT = 12 * float(np.log(2.0))
EXPONENT = 0x7F800000
TINY = 1e-30

PLAN = {
    8: dict(xs=0, xm=1, xh=1, xlo=2, xt=3, xst=4, last_xn=5, cv=(0, 2, 3, 4), fin=6, st=8,
            sq0=4, ss0=5, n0=6, hi0=6, lo0=7, h00=8, h01=9, h02=10,
            sq1=8, ss1=9, n1=10, hi1=11, lo1=11, lv0=7, lv1=14, h10=13, h11=14, h12=14,
            ld=5, res=11, ohi=6, olo=6, ot=7, op0a=10, op0b=11, op1a=12, op1b=13, a0=12, a1=14, yt=15),
    4: dict(xs=0, xm=0, xh=0, xlo=0, xt=1, xst=1, last_xn=2, cv=(0, 0, 1, 1), fin=2, st=3,
            sq0=2, ss0=2, n0=2, hi0=3, lo0=3, h00=3, h01=4, h02=4,
            sq1=4, ss1=4, n1=4, hi1=4, lo1=4, lv0=3, lv1=5, h10=7, h11=7, h12=7,
            ld=5, res=5, ohi=5, olo=5, ot=6, op0a=6, op0b=6, op1a=7, op1b=7, a0=7, a1=7, yt=7),
}


def need(eng, sem, count):
    if isinstance(count, int) and count <= 0:
        return
    eng.wait_ge(sem, count)


def dims(x, W_qkv):
    B, N, D = x.shape
    K = D // P
    assert N == D and K in PLAN and W_qkv.shape == (D, 3 * D)
    return B, N, D, K


def bass_cond_attention_conv(nc, x, cond, W_emb, b_emb, g_norm, W_qkv, g_q, g_k, W_out, b_conv, out):
    B, N, D, K = dims(x, W_qkv)
    U = B * K
    with ExitStack() as ctx:
        def sb(name, shape, dt):
            return ctx.enter_context(nc.sbuf_tensor(name, shape, dt))

        const = dict(
            eye32=sb("eye32", [P, P], F32), eye16=sb("eye16", [P, P], F16),
            wo=sb("wo", [P, K, 2, D], F16),
            eps_u=sb("eps_u", [P, U], F32),
            v_scale=sb("v_scale", [P, U], F32),
            y_scale=sb("y_scale", [P, U], F32),
            carry=sb("carry", [P, U], F32),
            g_qk=sb("g_qk", [P, DH], F32),
            l_scale=sb("l_scale", [P, 1], F32),
            taps=sb("taps", [P, B, K], F32), conv_b=sb("conv_b", [P, K], F32),
            power=sb("power", [P, 4 * K], F32),
        )
        w_dram = nc.dram_tensor("w_dram", [K, P, K, 2, 6 * DH], F16, kind="Internal").ap()
        xn_dram = nc.dram_tensor("xn_dram", [U, P, K * 2 * P], F16, kind="Internal").ap()
        o_dram = nc.dram_tensor("o_dram", [U * P, D], F32, kind="Internal").ap()
        mod_dram = nc.dram_tensor("mod_dram", [B, 2, K, P], F32, kind="Internal").ap()
        prepare(nc, const, w_dram, mod_dram, x, cond, W_emb, b_emb, g_norm, W_qkv, g_q, g_k, W_out, b_conv)
        main(nc, const, w_dram, mod_dram, xn_dram, o_dram, x, W_qkv, out)


def prepare(nc, const, w_dram, mod_dram, x, cond, W_emb, b_emb, g_norm, W_qkv, g_q, g_k, W_out, b_conv):
    B, N, D, K = dims(x, W_qkv)
    NE = 2 * D // 512
    rows = B * K + 4 * K
    row_embb, row_g, row_cb = B * K, B * K + 2 * K, B * K + 3 * K
    with ExitStack() as ctx:
        def sb(name, shape, dt):
            return ctx.enter_context(nc.sbuf_tensor(name, shape, dt))

        def psum(name, shape, dt):
            return ctx.enter_context(nc.psum_tensor(name, shape, dt))

        def sem(name):
            return ctx.enter_context(nc.semaphore(name))

        small = sb("small", [rows, P], F32)
        smallT = sb("smallT", [P, rows], F32)
        emb_w = sb("emb_w", [P, 2, 2 * D], F32)
        wq_raw = sb("wq_raw", [P, 3, 3 * D], F32)
        wq_pair = sb("wq_pair", [P, 2, K, 2, 6 * DH], F16)
        wo_raw = sb("wo_raw", [P, K, D], F32)
        ss_row = sb("ss_row", [B, 2 * D], F32)
        ssT = sb("ssT", [P, 2 * K, B], F32)
        mod = sb("mod", [P, 2, K, B], F32)
        wide = sb("wide", [P, B, 2, K], F32)
        mod_rows = sb("mod_rows", [B * 2 * K, P], F32)
        gq = sb("gq", [P, 2, DH], F32)
        wq_max = sb("wq_max", [P, K], F32)
        wq_two = sb("wq_two", [P, K], F32)
        wq_inv = sb("wq_inv", [P, K], F32)
        wo_max = sb("wo_max", [P, K], F32)
        wo_top = sb("wo_top", [P, 4], F32)
        top = sb("top", [P, B], F32)
        topr = sb("topr", [P, B], F32)
        two = sb("two", [P, B], F32)
        twoi = sb("twoi", [P, B], F32)
        gmax = sb("gmax", [P, 4], F32)
        tmpb = sb("tmpb", [P, 3, B], F32)
        ps_row = psum("ps_row", [B, 2 * D], F32)
        ps_t = psum("ps_t", [P, 512], F32)
        ps_s = psum("ps_s", [P, 512], F32)

        small_in = sem("small_in")
        g_in = sem("g_in")
        emb_in = [sem(f"emb_in{i}") for i in range(2)]
        wq_in = [sem(f"wq_in{i}") for i in range(3)]
        wo_in = [sem(f"wo_in{i}") for i in range(2)]
        wo_rows = sem("wo_rows")
        wo_all = sem("wo_all")
        mod_done = sem("mod_done")
        mod_t = sem("mod_t")
        mod_c = sem("mod_c")
        mod_out = sem("mod_out")
        wq_out = [sem(f"wq_out{i}") for i in range(2)]
        eye = sem("eye")
        eyed = sem("eyed")
        small_t = sem("small_t")
        small_c = sem("small_c")
        emb_mm = sem("emb_mm")
        emb_row = sem("emb_row")
        emb_t = sem("emb_t")
        dve = sem("dve_step")
        wq_scaled = sem("wq_scaled")
        wq_hi = sem("wq_hi")
        wq_lo = sem("wq_lo")
        wo_scaled = sem("wo_scaled")
        wo_hi = sem("wo_hi")
        top_in = sem("top_in")
        top_all = sem("top_all")
        emb_v = W_emb.rearrange("(c p) n -> c p n", p=P)
        wq_v = W_qkv.rearrange("(c p) n -> c p n", p=P)
        wo_v = W_out.rearrange("(c p) n -> c p n", p=P)
        block = ctx.enter_context(nc.Block())

        def store_wq(sp, c):
            sp.wait_ge(wq_hi, 3 * (c + 1))
            sp.wait_ge(wq_lo, c + 1)
            sp.dma_start(w_dram[:, :, c].rearrange("h p s n -> p h (s n)"),
                         wq_pair[:, c % 2].rearrange("p h s n -> p h (s n)")).then_inc(wq_out[c % 2], 16)

        def by_head(c, s, j):
            return wq_pair[:, c % 2, :, s, :].rearrange("p g (h j d) -> p g h j d", h=2, j=3)[:, :, :, j, :]

        def raw_by_head(c, j):
            return wq_raw[:, c % 3, j * D:(j + 1) * D].rearrange("p (g h d) -> p g h d", h=2, d=DH)

        @block.sync
        def _(sp):
            sp.dma_start(small[0:B * K, :], cond.rearrange("b (c p) -> (b c) p", p=P)).then_inc(small_in, 16)
            sp.dma_start(small[row_embb:row_g, :], b_emb.rearrange("(c p) -> c p", p=P)).then_inc(small_in, 16)
            sp.dma_start(small[row_g:row_cb, :], g_norm.rearrange("(c p) -> c p", p=P)).then_inc(small_in, 16)
            sp.dma_start(small[row_cb:rows, :], b_conv.rearrange("(c p) -> c p", p=P)).then_inc(small_in, 16)
            sp.dma_start(gq[:, 0, :], g_q.rearrange("(a d) -> a d", a=1).to_broadcast([P, DH])).then_inc(g_in, 16)
            sp.dma_start(gq[:, 1, :], g_k.rearrange("(a d) -> a d", a=1).to_broadcast([P, DH])).then_inc(g_in, 16)
            for c in range(K):
                need(sp, wo_in[c % 2], 16 * (c // 2))
                sp.dma_start(wo_raw[:, c, :], wo_v[c]).then_inc(wo_in[c % 2], 16)
            for c in range(K):
                need(sp, wq_lo, c - 2)
                sp.dma_start(wq_raw[:, c % 3, :], wq_v[c]).then_inc(wq_in[c % 3], 16)
                need(sp, emb_mm, c - 1)
                sp.dma_start(emb_w[:, c % 2, :], emb_v[c]).then_inc(emb_in[c % 2], 16)
                if c:
                    store_wq(sp, c - 1)
            store_wq(sp, K - 1)
            sp.wait_ge(mod_c, 1)
            sp.dma_start(mod_dram.rearrange("b i k p -> (b i k) p"), mod_rows[:]).then_inc(mod_out, 16)
            sp.wait_ge(mod_out, 16)
            sp.wait_ge(wq_out[0], 16 * (K // 2))
            sp.wait_ge(wq_out[1], 16 * (K // 2))

        @block.gpsimd
        def _(pool):
            nc.gpsimd.memset(const["eye32"][:], 0.0).then_inc(eye, 1)
            nc.gpsimd.memset(const["power"][:], -0.5)
            nc.gpsimd.memset(const["carry"][:], 1.0).then_inc(eye, 1)
            pool.wait_ge(eye, 2)
            nc.gpsimd.affine_select(out=const["eye32"][:], in_=const["eye32"][:], compare_op=ALU.not_equal,
                                    fill=1.0, base=0, pattern=[[-1, P]], channel_multiplier=1).then_inc(eye, 1)
            nc.gpsimd.memset(const["carry"][:].rearrange("p (b k) -> p b k", k=K)[:, :, 0:1], 0.0).then_inc(eye, 1)
            pool.wait_ge(eye, 4)
            nc.gpsimd.tensor_copy(const["eye16"][:], const["eye32"][:]).then_inc(eyed, 1)
            pool.wait_ge(wo_rows, 1)
            nc.gpsimd.partition_all_reduce(wo_top[:, 1:2], wo_top[:, 0:1], P, RMAX).then_inc(wo_all, 1)
            pool.wait_ge(top_in, 1)
            nc.gpsimd.partition_all_reduce(topr[:], top[:], P, RMAX).then_inc(top_all, 1)

        @block.scalar
        def _(act):
            act.wait_ge(wo_scaled, 1)
            for c in range(K):
                nc.scalar.activation(const["wo"][:, c, 0, :], wo_raw[:, c, :], ACT.Copy,
                                     scale=wo_top[:, 3:4]).then_inc(wo_hi, 1)
            for c in range(K):
                act.wait_ge(wq_scaled, c + 1)
                if c >= 2:
                    act.wait_ge(wq_out[c % 2], 16 * (c // 2))
                for j in range(3):
                    nc.scalar.activation(by_head(c, 0, j), raw_by_head(c, j), ACT.Copy,
                                         scale=wq_inv[:, c:c + 1]).then_inc(wq_hi, 1)
            act.wait_ge(emb_mm, K)
            nc.scalar.activation(ss_row[:], ps_row[:], ACT.Copy).then_inc(emb_row, 1)

        @block.tensor
        def _(pe):
            pe.wait_ge(small_in, 64)
            pe.wait_ge(eyed, 1)
            nc.tensor.transpose(ps_s[:, 0:rows], small[:], const["eye32"][0:rows, 0:rows]).then_inc(small_t, 1)
            pe.wait_ge(small_c, 1)
            cT = smallT[:, 0:B * K].rearrange("p (b c) -> p c b", c=K)
            for c in range(K):
                pe.wait_ge(emb_in[c % 2], 16 * (c // 2 + 1))
                for n in range(NE):
                    last = nc.tensor.matmul(ps_row[:, n * 512:(n + 1) * 512], cT[:, c, :],
                                            emb_w[:, c % 2, n * 512:(n + 1) * 512], start=(c == 0), stop=(c == K - 1))
                last.then_inc(emb_mm, 1)
            pe.wait_ge(emb_row, 1)
            for m in range(2 * K):
                last = nc.tensor.transpose(ps_t[:, m * B:(m + 1) * B], ss_row[:, m * P:(m + 1) * P],
                                           const["eye32"][0:B, 0:B])
            last.then_inc(emb_t, 1)
            pe.wait_ge(mod_done, 1)
            nc.tensor.transpose(ps_s[0:B * 2 * K, 0:P], wide[:].rearrange("p b i k -> p (b i k)"),
                                const["eye32"][:]).then_inc(mod_t, 1)

        @block.vector
        def _(v):
            steps = [0]

            def step(ins):
                steps[0] += 1
                ins.then_inc(dve, 1)
                v.wait_ge(dve, steps[0])

            def power_of_two(out, in_):
                step(nc.vector.tensor_scalar(in_, in_, TINY, None, ALU.max))
                step(nc.vector.tensor_scalar(out.bitcast(U32), in_.bitcast(U32), EXPONENT, None, ALU.bitwise_and))

            v.wait_ge(small_t, 1)
            nc.vector.tensor_copy(smallT[:], ps_s[:, 0:rows]).then_inc(small_c, 1)
            v.wait_ge(g_in, 32)
            step(nc.vector.tensor_tensor(const["g_qk"][:], gq[:, 0, :], gq[:, 1, :], ALU.mult))
            step(nc.vector.tensor_reduce(gmax[:, 0:1], const["g_qk"][:], axis=AX.X, op=ALU.max,
                                         apply_absolute_value=True))
            power_of_two(gmax[:, 1:2], gmax[:, 0:1])
            step(nc.vector.reciprocal(gmax[:, 2:3], gmax[:, 1:2]))
            step(nc.vector.tensor_scalar(const["g_qk"][:], const["g_qk"][:], gmax[:, 2:3], None, ALU.mult))
            step(nc.vector.tensor_scalar(const["l_scale"][:], gmax[:, 1:2], DH ** -0.5 / QK_UP ** 2, None, ALU.mult))
            for c in range(K):
                v.wait_ge(wo_in[c % 2], 16 * (c // 2 + 1))
                step(nc.vector.tensor_reduce(wo_max[:, c:c + 1], wo_raw[:, c, :], axis=AX.X, op=ALU.max,
                                             apply_absolute_value=True))
            nc.vector.tensor_reduce(wo_top[:, 0:1], wo_max[:], axis=AX.X, op=ALU.max).then_inc(wo_rows, 1)
            v.wait_ge(wo_all, 1)
            power_of_two(wo_top[:, 2:3], wo_top[:, 1:2])
            step(nc.vector.reciprocal(wo_top[:, 3:4], wo_top[:, 2:3]))
            nc.vector.tensor_scalar(wo_top[:, 3:4], wo_top[:, 3:4], W_UP, None, ALU.mult).then_inc(wo_scaled, 1)
            v.wait_ge(wo_scaled, 1)
            for c in range(K):
                v.wait_ge(wo_hi, c + 1)
                nc.vector.scalar_tensor_tensor(out=const["wo"][:, c, 1, :], in0=wo_raw[:, c, :], scalar=wo_top[:, 3:4],
                                               in1=const["wo"][:, c, 0, :], op0=ALU.mult, op1=ALU.subtract)
            for c in range(K):
                v.wait_ge(wq_in[c % 3], 16 * (c // 3 + 1))
                step(nc.vector.tensor_reduce(wq_max[:, c:c + 1], wq_raw[:, c % 3, :], axis=AX.X, op=ALU.max,
                                             apply_absolute_value=True))
                power_of_two(wq_two[:, c:c + 1], wq_max[:, c:c + 1])
                step(nc.vector.reciprocal(wq_inv[:, c:c + 1], wq_two[:, c:c + 1]))
                nc.vector.tensor_scalar(wq_inv[:, c:c + 1], wq_inv[:, c:c + 1], W_UP, None,
                                        ALU.mult).then_inc(wq_scaled, 1)
                v.wait_ge(wq_scaled, c + 1)
                for j in range(3):
                    v.wait_ge(wq_hi, 3 * c + j + 1)
                    for h in range(2):
                        last = nc.vector.scalar_tensor_tensor(
                            out=by_head(c, 1, j)[:, :, h, :], in0=raw_by_head(c, j)[:, :, h, :],
                            scalar=wq_inv[:, c:c + 1], in1=by_head(c, 0, j)[:, :, h, :],
                            op0=ALU.mult, op1=ALU.subtract)
                last.then_inc(wq_lo, 1)
            v.wait_ge(emb_t, 1)
            step(nc.vector.tensor_tensor(
                ssT[:], ps_t[:, 0:2 * K * B].rearrange("p (m b) -> p m b", b=B),
                smallT[:, row_embb:row_g].rearrange("p (m a) -> p m a", a=1).to_broadcast([P, 2 * K, B]), ALU.add))
            step(nc.vector.tensor_scalar(mod[:, 0], ssT[:, 0:K, :], 1.0, None, ALU.add))
            step(nc.vector.tensor_tensor(
                mod[:, 0], mod[:, 0],
                smallT[:, row_g:row_cb].rearrange("p (m a) -> p m a", a=1).to_broadcast([P, K, B]), ALU.mult))
            step(nc.vector.tensor_copy(mod[:, 1], ssT[:, K:2 * K, :]))
            for i in range(2):
                step(nc.vector.tensor_tensor(
                    mod[:, i], mod[:, i], wq_two[:].rearrange("p (m a) -> p m a", a=1).to_broadcast([P, K, B]),
                    ALU.mult))
            for b in range(B):
                step(nc.vector.tensor_reduce(top[:, b:b + 1], mod[:, :, :, b], axis=AX.XY, op=ALU.max,
                                             apply_absolute_value=True))
            nc.vector.memset(gmax[:, 3:4], 0.0).then_inc(top_in, 1)
            v.wait_ge(top_all, 1)
            power_of_two(two[:], topr[:])
            step(nc.vector.reciprocal(twoi[:], two[:]))
            step(nc.vector.tensor_scalar(tmpb[:, 0], twoi[:, 0:B], X_UP, None, ALU.mult))
            for i in range(2):
                step(nc.vector.tensor_tensor(
                    wide[:, :, i, :].rearrange("p b k -> p k b"), mod[:, i],
                    tmpb[:, 0].rearrange("p (a b) -> p a b", a=1).to_broadcast([P, K, B]), ALU.mult))
            nc.vector.memset(gmax[:, 3:4], 1.0).then_inc(mod_done, 1)
            v.wait_ge(mod_t, 1)
            nc.vector.tensor_copy(mod_rows[:], ps_s[0:B * 2 * K, 0:P]).then_inc(mod_c, 1)
            down = 1.0 / (X_UP * W_UP * QKV_DOWN)
            step(nc.vector.tensor_scalar(tmpb[:, 1], two[:, 0:B], down, None, ALU.mult))

            def by_unit(name):
                return const[name][:].rearrange("p (b k) -> p b k", k=K)

            def column(ap):
                return ap.rearrange("p (b a) -> p b a", a=1).to_broadcast([P, B, K])

            step(nc.vector.tensor_copy(by_unit("v_scale"), column(tmpb[:, 1])))
            step(nc.vector.tensor_tensor(tmpb[:, 2], twoi[:, 0:B], twoi[:, 0:B], ALU.mult))
            step(nc.vector.tensor_scalar(tmpb[:, 2], tmpb[:, 2], EPS / down ** 2 / QK_UP ** 2, None, ALU.mult))
            step(nc.vector.tensor_copy(by_unit("eps_u"), column(tmpb[:, 2])))
            step(nc.vector.tensor_scalar(tmpb[:, 1], tmpb[:, 1], wo_top[:, 2:3], 1.0 / W_UP, ALU.mult, ALU.mult))
            step(nc.vector.tensor_copy(by_unit("y_scale"), column(tmpb[:, 1])))
            step(nc.vector.tensor_copy(const["taps"][:], smallT[:, 0:B * K].rearrange("p (b c) -> p b c", c=K)))
            step(nc.vector.tensor_scalar(const["taps"][:, B - 1, :], const["taps"][:, B - 1, :], 1.0, None, ALU.add))
            step(nc.vector.tensor_copy(const["conv_b"][:], smallT[:, row_cb:rows]))


def main(nc, const, w_dram, mod_dram, xn_dram, o_dram, x, W_qkv, out):
    B, N, D, K = dims(x, W_qkv)
    U = B * K
    NS = 2 * K
    EARLY = min(4, K - 1)
    KH = K // 2
    HC = K // 2
    HW = HC * P
    HN = N // 2
    LEAD = K
    G = NS // 4
    TAPS = B
    H = TAPS - 1
    at = PLAN[K]
    x_t = x.rearrange("b n d -> (b n) d")
    out_t = out.rearrange("b n d -> (b n) d")
    with ExitStack() as ctx:
        def sb(name, shape, dt):
            return ctx.enter_context(nc.sbuf_tensor(name, shape, dt))

        def psum(name, shape, dt):
            return ctx.enter_context(nc.psum_tensor(name, shape, dt))

        def sem(name):
            return ctx.enter_context(nc.semaphore(name))

        w_sb = sb("w_sb", [P, 2, K, 2, 6 * DH], F16)
        xn_sb = sb("xn_sb", [P, 4, 2 * K, P], F16)
        stage = sb("stage", [P, 2, 2 * KH, 3 * DH], F32)
        square = sb("square", [P, 4 * KH * DH], F32)
        q_pair = sb("q_pair", [P, 2 * KH, 2 * DH], F16)
        k_pair = sb("k_pair", [P, 2 * KH, 3 * DH], F16)
        stack = sb("stack", [P, 2, 2, 3, N], F16)
        v_pair = sb("v_pair", [P, 2, 2 * K, 2 * DH], F16)
        prob = sb("prob", [P, 4, N], F32)
        p_pair = sb("p_pair", [P, 4, 2, N], F16)
        pT = sb("pT", [P, 4, 2 * K, P], F16)
        o_lo = sb("o_lo", [P, 4, DH], F32)
        o_out = sb("o_out", [P, K, 2, DH], F32)
        y = sb("y", [P, D], F32)
        o_in = sb("o_in", [P, D], F32)
        pair = sb("pair", [P, 2, D], F16)
        rows = sb("rows", [P, 2, D], F32)
        pairT = sb("pairT", [P, 2 * K, P], F16)
        yT = sb("yT", [P, K, H + P], F32)
        acc = sb("acc", [P, K, P], F32)
        fin = sb("fin", [P, D], F32)
        x_in = sb("x_in", [P, D], F32)
        neg = sb("neg", [P, NS], F32)
        bias = sb("bias", [P, NS], F32)
        total = sb("total", [P, 2 * NS], F32)
        inv = sb("inv", [P, 4], F32)
        ms = sb("ms", [P, 4 * KH], F32)
        rs = sb("rs", [P, 4 * KH], F32)
        msx = sb("msx", [P, 4, 3], F32)

        scores = psum("scores", [P, 2, max(N, 1024)], F32)
        values = psum("values", [P, 2, 4, 2 * DH], F32)
        misc = psum("misc", [P, 2, 512], F32)

        gate = sem("gate")
        w_in = [sem(f"w_in{i}") for i in range(4)]
        xn_in = [sem(f"xn_in{i}") for i in range(4)]
        rows_in = sem("rows_in")
        first_x_ld = [sem(f"first_x_ld{i}") for i in range(4)]
        x_ld = sem("x_ld")
        x_sq = sem("x_sq")
        x_ms = sem("x_ms")
        x_pw = sem("x_pw")
        x_mul = sem("x_mul")
        x_mod = sem("x_mod")
        x_hi = sem("x_hi")
        x_lo = sem("x_lo")
        first_xT_in = [sem(f"first_xT_in{i}") for i in range(2)]
        xT_in = sem("xT_in")
        x_st = sem("x_st")
        qkv_mm = sem("qkv_mm")
        qkv_ev = sem("qkv_ev")
        h_sq = sem("h_sq")
        h_ss = sem("h_ss")
        h_ms = sem("h_ms")
        h_pw = sem("h_pw")
        h_n = sem("h_n")
        h_hi = sem("h_hi")
        h_lo = sem("h_lo")
        h_tr = sem("h_tr")
        h_ev = sem("h_ev")
        qk_done = sem("qk_done")
        max_done = sem("max_done")
        bias_done = sem("bias_done")
        exp_done = sem("exp_done")
        hi_done = sem("hi_done")
        lo_done = sem("lo_done")
        pT_in = [sem(f"pT_in{i}") for i in range(4)]
        pv_done = sem("pv_done")
        ov_copy = sem("ov_copy")
        ov_add = sem("ov_add")
        ov_inv = sem("ov_inv")
        ov_done = sem("ov_done")
        o_st = sem("o_st")
        o_ld = sem("o_ld")
        xo_ld = sem("xo_ld")
        last_o_ld = [sem(f"last_o_ld{i}") for i in range(2)]
        last_x_ld = [sem(f"last_x_ld{i}") for i in range(2)]
        o_hi = sem("o_hi")
        o_low = sem("o_low")
        oT_in = sem("oT_in")
        last_oT_in = [sem(f"last_oT_in{i}") for i in range(2)]
        s_done = sem("s_done")
        op_mm = sem("op_mm")
        op_ev = sem("op_ev")
        y_tr = sem("y_tr")
        y_ev = sem("y_ev")
        halo = sem("halo")
        cv = sem("cv")
        f_tr = sem("f_tr")
        f_ev = sem("f_ev")
        f_st = sem("f_st")
        block = ctx.enter_context(nc.Block())

        stack_banks = ((0, 1, 0), (1, 0, 1))

        def in_units(eng, unit, load_rows=None):
            def pairs(lo, hi, **parts):
                if lo < hi:
                    with eng.Fori(lo // 2, hi // 2) as j:
                        for parity in range(2):
                            unit(2 * j + parity, parity, **parts)

            def next_rows(b):
                if load_rows:
                    load_rows(b)

            assert B >= 3
            next_rows(1)
            unit(0, 0, qkv=True, xs=True, outs=False, fins=False)
            unit(1, 1, qkv=True, xs=True, outs=False, fins=False)
            pairs(2, K, qkv=True, xs=True, outs=False, fins=False)
            next_rows(2)
            unit(K, 0, qkv=True, xs=True, outs=True, fins=False)
            unit(K + 1, 1, qkv=True, xs=True, outs=True, fins=True)
            pairs(K + 2, 2 * K, qkv=True, xs=True, outs=True, fins=True)
            for b in range(2, B - 1):
                next_rows(b + 1)
                pairs(b * K, (b + 1) * K, qkv=True, xs=True, outs=True, fins=True)
            pairs(U - K, U - 2, qkv=True, xs=False, outs=True, fins=True)
            unit(U - 2, 0, qkv=True, xs=False, outs=True, fins=True)
            unit(U - 1, 1, qkv=False, xs=False, outs=True, fins=True)

        def in_last_tiles(eng, tile):
            tile(U - K, 0, first=True, last=False)
            tile(U - K + 1, 1, first=False, last=False)
            if K > 4:
                with eng.Fori((U - K) // 2 + 1, U // 2 - 1) as j:
                    for parity in range(2):
                        tile(2 * j + parity, parity, first=False, last=False)
            tile(U - 2, 0, first=False, last=False)
            tile(U - 1, 1, first=False, last=True)

        def half_bank(psum_banks, hh):
            return psum_banks[:, hh * 512:hh * 512 + HW]

        last_values = values[:].rearrange("p a s n -> p (a s n)")
        last_banks = dict(y=[half_bank(scores[:, 1], hh) for hh in range(2)],
                          f=[half_bank(last_values, hh) for hh in range(2)])
        y_banks = [misc[:, 0, 0:HW], misc[:, 1, 0:HW]]
        f_banks = y_banks
        last_o_in = [prob[:, i, 0:D] for i in range(2)]
        last_pair = [p_pair[:, i] for i in range(2)]
        last_oT = [pT[:, i] for i in range(2)]
        first_x = [prob[:, i, 0:D] for i in range(4)]
        first_pair = [p_pair[:, i] for i in range(4)]
        first_xT = [pT[:, i] for i in range(4)]
        last_y = [prob[:, 2 + i, 0:D] for i in range(2)]

        def last_loads(T, par):
            return 8 * (T - par - (U - K)) + 16

        def group(u, s):
            if isinstance(u, int) and NS * u + s < 8:
                return None
            return (G * u + s // 4 - 2, (s // 4) % 2)

        def four(u, s):
            return G * u + s // 4

        def slot(u, s):
            return NS * u + s

        @block.sync
        def _(sp):
            def passed():
                sp.sem_inc(gate, 1)

            def load_rows(b):
                need(sp, x_mod, K * b)
                sp.dma_start(rows[:].rearrange("p i n -> p (i n)"),
                             mod_dram[b].rearrange("(a i) k p -> a (i k p)", a=1).to_broadcast([P, 2 * D])
                             ).then_inc(rows_in, 16)

            def load_x(v, buffer, free, done):
                need(sp, x_lo, free)
                sp.dma_start(buffer, x_t[bass.ds(v * P, P), :]).then_inc(done, 16)

            def transpose_x(v, pair_, xT_, free, done):
                sp.wait_ge(x_lo, v + 1)
                passed()
                need(sp, x_st, free)
                passed()
                sp.dma_start_transpose(xT_, pair_.rearrange("p a n -> p (a n)")).then_inc(done, 16)

            def store_xn(v, xT_, done, count):
                sp.wait_ge(done, count)
                need(sp, x_st, 16 * v)
                sp.dma_start(xn_dram[bass.ds(v, 1)].rearrange("a p n -> (a p) n"),
                             xT_.rearrange("p c n -> p (c n)")).then_inc(x_st, 16)

            def load_w(w, par, i):
                need(sp, qkv_mm, K * (w - 1) + 1)
                cs = slice(i * K // 4, (i + 1) * K // 4)
                sp.dma_start(w_sb[:, par, cs].rearrange("p c s n -> p (c s n)"),
                             w_dram[bass.ds(w % K, 1), :, cs].rearrange("a p c s n -> (a p) (c s n)")
                             ).then_inc(w_in[i], 16)

            def load_xn(w, t):
                need(sp, qkv_mm, K * w + t - 3)
                need(sp, x_st, 16 * ((w // K) * K + t + 1))
                sp.dma_start(xn_sb[:, t % 4].rearrange("p c n -> p (c n)"),
                             xn_dram[bass.ds((w // K) * K + t, 1)].rearrange("a p n -> (a p) n")
                             ).then_inc(xn_in[t % 4], 16)

            def transpose_p(u, s):
                g = slot(u, s)
                sp.wait_ge(lo_done, g + 1)
                passed()
                need(sp, pv_done, g - 3)
                passed()
                sp.dma_start_transpose(pT[:, s % 4], p_pair[:, s % 4].rearrange("p a n -> p (a n)")
                                       ).then_inc(pT_in[s % 4], 16)

            def store_o(u, lo=0, hi=K):
                sp.wait_ge(ov_done, G * u + G - (K - hi) // 4)
                sp.dma_start(
                    o_dram[bass.ds((u // K) * K * P + lo * P, (hi - lo) * P), bass.ds((u % K) * P, P)].rearrange(
                        "(t p) n -> p t n", p=P),
                    o_out[:, lo:hi].rearrange("p t h d -> p t (h d)")).then_inc(o_st, 16)

            def load_out(T):
                sp.wait_ge(o_st, 16 * ((T // K) * K + K))
                need(sp, o_low, T)
                need(sp, s_done, T)
                sp.dma_start(o_in[:], o_dram[bass.ds(T * P, P), :]).then_inc(o_ld, 16)

            def transpose_o(T, pair_, oT_, done):
                sp.wait_ge(o_low, T + 1)
                passed()
                sp.dma_start_transpose(oT_, pair_.rearrange("p a n -> p (a n)")).then_inc(done, 16)

            def load_xo(T):
                need(sp, y_tr, 2 * T)
                sp.dma_start(y[:], x_t[bass.ds(T * P, P), :]).then_inc(xo_ld, 16)

            def store_out(T):
                sp.wait_ge(f_ev, 2 * T + 2)
                sp.dma_start(out_t[bass.ds(T * P, P), :], fin[:]).then_inc(f_st, 16)

            def unit(u, par, qkv, xs, outs, fins):
                w, v, T = u + 1, u + LEAD, u - K
                more = qkv and not (isinstance(u, int) and u + 2 >= U)
                for s in range(NS):
                    g2 = s - 2
                    if g2 >= 0:
                        transpose_p(u, g2)
                    elif not (isinstance(u, int) and u == 0):
                        transpose_p(u - 1, NS + g2)
                    if qkv and s and EARLY - 1 + s < K - 1:
                        load_xn(w, EARLY - 1 + s)
                    if xs and s == at["xt"]:
                        if fins:
                            sp.wait_ge(op_mm, 2 * T)
                            passed()
                        transpose_x(v, pair, pairT[:], 16 * v, xT_in)
                    if xs and s == at["xst"]:
                        store_xn(v, pairT[:], xT_in, 16 * (u + 1))
                    if qkv and s == at["last_xn"]:
                        load_xn(w, K - 1)
                    if xs and s == K and not (isinstance(u, int) and v + 1 >= U):
                        load_x((v + 1) % U, x_in[:], v + 1, x_ld)
                    if more and K < s <= K + EARLY:
                        load_xn(w + 1, s - K - 1)
                    if more and s >= K and (s - K) % (K // 4) == 0:
                        load_w(w + 1, par, (s - K) // (K // 4))
                    if s == 5 % NS and not (isinstance(u, int) and u == 0):
                        store_o(u - 1)
                    if outs and s == at["ld"]:
                        load_xo(T)
                        load_out(T)
                    if outs and s == at["ot"]:
                        need(sp, op_mm, 2 * T)
                        passed()
                        if xs:
                            sp.wait_ge(x_st, 16 * (v + 1))
                            passed()
                        transpose_o(T, pair, pairT[:], oT_in)
                    if fins and s == at["st"]:
                        store_out(T - 1)

            def load_last_y(T, par):
                need(sp, y_tr, 2 * T - 2)
                sp.dma_start(last_y[par], x_t[bass.ds(T * P, P), :]).then_inc(last_x_ld[par], 16)

            def load_last_o(T, par):
                sp.wait_ge(o_low, T - 1)
                sp.wait_ge(s_done, T - 1)
                sp.dma_start(last_o_in[par], o_dram[bass.ds(T * P, P), :]).then_inc(last_o_ld[par], 16)

            def transpose_last(T, par):
                need(sp, op_mm, 2 * T - 2)
                passed()
                transpose_o(T, last_pair[par], last_oT[par], last_oT_in[par])

            def last_tile(T, par, first, last):
                if not last:
                    transpose_last(T + 1, 1 - par)
                if not (isinstance(T, int) and T + 2 >= U):
                    load_last_o(T + 2, par)
                if not last:
                    load_last_y(T + 1, 1 - par)
                store_out(T - 1)

            def first_store(v):
                store_xn(v, first_xT[v % 4], first_xT_in[v % 2], 16 * (v // 2 + 1))

            for v in range(4):
                load_x(v, first_x[v], 0, first_x_ld[v])
                if v == 0:
                    load_rows(0)
            for i in range(4):
                load_w(0, 0, i)
            load_x(LEAD, x_in[:], 0, x_ld)
            for v in range(LEAD):
                need(sp, qkv_mm, v - 3)
                transpose_x(v, first_pair[v % 4], first_xT[v % 4], 16 * (v - 3), first_xT_in[v % 2])
                if v + 4 < LEAD:
                    load_x(v + 4, first_x[v % 4], v + 1, first_x_ld[v % 4])
                if v:
                    first_store(v - 1)
            first_store(LEAD - 1)
            for i in range(4):
                load_w(1, 1, i)
            for t in range(EARLY):
                load_xn(1, t)
            in_units(sp, unit, load_rows)
            transpose_p(U - 1, NS - 2)
            transpose_p(U - 1, NS - 1)
            store_o(U - 1, 0, 4)
            sp.wait_ge(o_st, 16 * U)
            load_last_o(U - K, 0)
            load_last_y(U - K, 0)
            if K > 4:
                store_o(U - 1, 4, K)
            sp.wait_ge(pv_done, NS * U)
            transpose_last(U - K, 0)
            sp.wait_ge(o_st, 16 * (U + (K > 4)))
            load_last_o(U - K + 1, 1)
            in_last_tiles(sp, last_tile)
            store_out(U - 1)
            sp.wait_ge(f_st, 16 * U)

        @block.tensor
        def _(pe):
            def bank(i):
                return misc[:, i]

            def f16_bank(i):
                return misc[:, i].bitcast(F16).rearrange("p (a n) -> p a n", a=2)

            def qk(u, s, par):
                h, qt = s // K, s % K
                need(pe, exp_done, slot(u, s) - 1)
                for n in range(2):
                    for i in range(2):
                        last = nc.tensor.matmul(scores[:, s % 2, n * HN:(n + 1) * HN],
                                                stack[:, par, h, 0, qt * P:(qt + 1) * P],
                                                stack[:, par, h, 1 + i, n * HN:(n + 1) * HN],
                                                start=(i == 0), stop=(i == 1))
                last.then_inc(qk_done, 1)

            def pv(u, s, par):
                h = s // K
                g = slot(u, s)
                if s % 4 == 0:
                    need(pe, ov_done, four(u, s) - 1)
                pe.wait_ge(pT_in[s % 4], 16 * (four(u, s) + 1))
                o = values[:, (s // 4) % 2, s % 4, :]
                for t in range(K - 1):
                    nc.tensor.matmul(o, pT[:, s % 4, t, :], v_pair[:, par, 2 * t + h, :],
                                     start=(t == 0), stop=False)
                for t in range(K):
                    nc.tensor.matmul(o[:, 0:DH], pT[:, s % 4, K + t, :], v_pair[:, par, 2 * t + h, 0:DH],
                                     start=False, stop=False)
                last = nc.tensor.matmul(o, pT[:, s % 4, K - 1, :], v_pair[:, par, 2 * (K - 1) + h, :],
                                        start=False, stop=True)
                last.then_inc(pv_done, 1)

            def project(w, par, t, xn, loaded, before=None):
                if t >= 2:
                    pe.wait_ge(qkv_ev, K * w + t - 1)
                if before:
                    pe.wait_ge(*before)
                pe.wait_ge(*loaded)
                acc_ = bank(t % 2)[:, 0:6 * DH]
                for c in range(K):
                    if t == 0 and c % (K // 4) == 0:
                        pe.wait_ge(w_in[c // (K // 4)], 16 * (w + 1))
                    for i, j in ((0, 0), (0, 1), (1, 0)):
                        last = nc.tensor.matmul(acc_, xn[:, i * K + c, :], w_sb[:, par, c, j, :],
                                                start=(c == 0 and i == j == 0), stop=(c == K - 1 and i == 1))
                last.then_inc(qkv_mm, 1)

            def stacks(w, hf, i, before):
                pe.wait_ge(h_lo, 3 * (2 * w + hf) + 2)
                pe.wait_ge(h_hi, 3 * (2 * w + hf) + 2)
                need(pe, *before)
                b = stack_banks[hf][i]
                for t in range(KH):
                    for a in range(2):
                        src = ((q_pair[:, 2 * t + i, :] if a == 0 else k_pair[:, 2 * t + i, 0:2 * DH])
                               if i < 2 else k_pair[:, 2 * t + a, DH:3 * DH])
                        last = nc.tensor.transpose(f16_bank(b)[:, a, t * P:(t + 1) * P], src, const["eye16"][:])
                last.then_inc(h_tr, 1)

            def transposes(dst, src, done):
                for c in range(HC):
                    last = nc.tensor.transpose(dst[:, c * P:(c + 1) * P], src(c), const["eye32"][:])
                last.then_inc(done, 1)

            def out_product(T, n, part, oT_, loaded, before=None):
                pe.wait_ge(*loaded)
                if before:
                    pe.wait_ge(*before)
                for c in range(part * HC, (part + 1) * HC):
                    for i, j in ((0, 0), (0, 1), (1, 0)):
                        last = nc.tensor.matmul(bank(1 - n)[:, 0:HN], oT_[:, i * K + c, :],
                                                const["wo"][:, c, j, n * HN:(n + 1) * HN],
                                                start=(c == 0 and i == j == 0), stop=(c == K - 1 and i == 1))
                if part == 1:
                    last.then_inc(op_mm, 1)

            def y_transposes(T, hh, banks, src, before):
                pe.wait_ge(op_ev, 2 * T + hh + 1)
                need(pe, *before)
                transposes(banks[hh], lambda c: src[:, (hh * HC + c) * P:(hh * HC + c + 1) * P], y_tr)

            def out_transposes(T, hh, banks, before):
                pe.wait_ge(cv, TAPS * K * T + TAPS * HC * (hh + 1))
                need(pe, *before)
                transposes(banks[hh], lambda c: acc[:, hh * HC + c, :], f_tr)

            def unit(u, par, qkv, xs, outs, fins):
                w, T = u + 1, u - K
                f = at["fin"]
                o_ready = (oT_in, 16 * (T + 1))
                for s in range(NS):
                    if s == 0:
                        pe.wait_ge(h_ev, 6 * (u + 1))
                    qk(u, s, par)
                    if fins and s == f:
                        out_transposes(T - 1, 0, f_banks, (qkv_ev, K * w + f - 1) if qkv else (y_ev, 2 * T))
                    if qkv and s == at["h01"]:
                        stacks(w, 0, 1, (qkv_ev, K * w + K))
                    if outs and s == at["op1b"] != at["op1a"]:
                        out_product(T, 1, 1, pairT, o_ready)
                    if s >= LAG:
                        pv(u, s - LAG, par)
                    elif not (isinstance(u, int) and u == 0):
                        pv(u - 1, NS + s - LAG, 1 - par)
                    if fins and s == f:
                        out_transposes(T - 1, 1, f_banks, (qkv_ev, K * w + f) if qkv else (y_ev, 2 * T))
                    if qkv and s < K:
                        before = None
                        if fins and s < 2:
                            before = (y_ev, 2 * T - 1 + s)
                        if fins and f <= s < f + 2:
                            before = (f_ev, 2 * T - 1 + s - f)
                        project(w, 1 - par, s, xn_sb[:, s % 4],
                                (xn_in[s % 4], 16 * (K // 4 * (w - 1) + s // 4 + 1)), before)
                    if qkv and s == at["h00"]:
                        stacks(w, 0, 0, (qkv_ev, K * w + K - 1))
                    if qkv and s == at["h02"]:
                        stacks(w, 0, 2, (h_ev, 6 * w + 1))
                    if outs and s == at["op0a"]:
                        out_product(T, 0, 0, pairT, o_ready, (h_ev, 6 * w + 2) if qkv else (f_ev, 2 * T))
                    if outs and s == at["op0b"]:
                        out_product(T, 0, 1, pairT, o_ready)
                    if outs and s == at["op1a"]:
                        out_product(T, 1, 0, pairT, o_ready, (h_ev, 6 * w + 3) if qkv else (f_ev, 2 * T))
                    if outs and s == at["op1b"] == at["op1a"]:
                        out_product(T, 1, 1, pairT, o_ready)
                    if qkv and s == at["h10"]:
                        stacks(w, 1, 0, (op_ev, 2 * T + 1) if outs else (h_ev, 6 * w + 2))
                    if qkv and s == at["h11"]:
                        stacks(w, 1, 1, (op_ev, 2 * T + 2) if outs else (h_ev, 6 * w + 3))
                    if qkv and s == at["h12"]:
                        stacks(w, 1, 2, (h_ev, 6 * w + 4))
                    if outs and s == at["yt"]:
                        y_transposes(T, 0, y_banks, y, (h_ev, 6 * w + 5) if qkv else (op_ev, 2 * T + 2))
                        y_transposes(T, 1, y_banks, y, (h_ev, 6 * w + 6) if qkv else (op_ev, 2 * T + 2))

            def last_tile(T, par, first, last):
                o_ready = (last_oT_in[par], last_loads(T, par))
                out_product(T, 0, 0, last_oT[par], o_ready, (y_ev, 2 * T) if first else (op_ev, 2 * T - 1))
                out_product(T, 0, 1, last_oT[par], o_ready)
                if not first:
                    y_transposes(T - 1, 1, last_banks["y"], last_y[1 - par], (y_ev, 2 * T - 2))
                out_product(T, 1, 0, last_oT[par], o_ready, (y_ev, 2 * T) if first else (op_ev, 2 * T))
                out_product(T, 1, 1, last_oT[par], o_ready)
                y_transposes(T, 0, last_banks["y"], last_y[par], (exp_done, NS * U) if first else (y_ev, 2 * T - 1))
                for hh in range(2):
                    out_transposes(T - 1, hh, last_banks["f"],
                                   (ov_done, G * U) if first else (f_ev, 2 * T - 3 + hh))

            for t in range(K):
                project(0, 0, t, first_xT[t % 4], (first_xT_in[t % 2], 16 * (t // 2 + 1)))
            for hf, before in enumerate((((qkv_ev, K - 1), (qkv_ev, K), (h_ev, 1)),
                                         ((h_ev, 2), (h_ev, 3), (h_ev, 4)))):
                for i in range(3):
                    stacks(0, hf, i, before[i])
            in_units(pe, unit)
            for s in range(NS - LAG, NS):
                pv(U - 1, s, 1)
            in_last_tiles(pe, last_tile)
            y_transposes(U - 1, 1, last_banks["y"], last_y[1], (y_ev, 2 * U - 2))
            for hh in range(2):
                out_transposes(U - 1, hh, last_banks["f"], (f_ev, 2 * U - 3 + hh))

        @block.scalar
        def _(act):
            def exponent(u, s, par):
                g = slot(u, s)
                act.wait_ge(bias_done, g + 1)
                need(act, lo_done, g - 3)
                if s % 4 == 0:
                    need(act, ov_inv, four(u, s) - 7)
                nc.scalar.activation(prob[:, s % 4, :], scores[:, s % 2, 0:N], ACT.Exp, bias=bias[:, s:s + 1],
                                     scale=const["l_scale"][:, 0:1],
                                     accum_out=total[:, par * NS + s:par * NS + s + 1]).then_inc(exp_done, 1)

            def read_projection(w, t):
                hf = t // KH
                act.wait_ge(qkv_mm, K * w + t + 1)
                if t % KH == 0:
                    need(act, h_lo, 3 * (2 * (w - 1) + hf + 1))
                nc.scalar.activation(stage[:, hf, 2 * (t % KH):2 * (t % KH) + 2, :],
                                     misc[:, t % 2, 0:6 * DH].rearrange("p (h n) -> p h n", h=2), ACT.Copy,
                                     scale=QKV_DOWN).then_inc(qkv_ev, 1)

            def squares(w, hf):
                act.wait_ge(qkv_ev, K * w + (hf + 1) * KH)
                need(act, h_ss, 2 * w + hf)
                nc.scalar.activation(square[:].rearrange("p (t n) -> p t n", n=2 * DH),
                                     stage[:, hf, :, 0:2 * DH], ACT.Square).then_inc(h_sq, 1)

            def high_halves(w, par, hf):
                act.wait_ge(h_n, 2 * (2 * w + hf) + 2)
                need(act, h_tr, 3 * (2 * w + hf))
                nc.scalar.activation(q_pair[:, :, 0:DH], stage[:, hf, :, 0:DH], ACT.Copy).then_inc(h_hi, 1)
                kk = k_pair[:].rearrange("p t (a d) -> p t a d", d=DH)
                for a in (0, 2):
                    last = nc.scalar.activation(kk[:, :, a, :], stage[:, hf, :, DH:2 * DH], ACT.Copy)
                last.then_inc(h_hi, 1)
                need(act, pv_done, NS * (w - 1))
                nc.scalar.activation(v_pair[:, par, 2 * KH * hf:2 * KH * (hf + 1), 0:DH],
                                     stage[:, hf, :, 2 * DH:3 * DH], ACT.Copy).then_inc(h_hi, 1)

            def read_stacks(w, par, hf, i):
                act.wait_ge(h_tr, 3 * (2 * w + hf) + i + 1)
                dst = stack[:, par, i, 0:2, hf * HN:(hf + 1) * HN] if i < 2 else \
                    stack[:, par, :, 2, hf * HN:(hf + 1) * HN]
                b = stack_banks[hf][i]
                nc.scalar.activation(dst, misc[:, b].bitcast(F16).rearrange("p (a n) -> p a n", a=2)[:, :, 0:HN],
                                     ACT.Copy).then_inc(h_ev, 1)

            def x_square(v, i, ring, buffer, loaded, ss_count):
                act.wait_ge(*loaded)
                need(act, h_ss, ss_count)
                need(act, x_ms, v - ring + 1)
                need(act, x_sq, v)
                nc.scalar.activation(square[:, 0:D].bitcast(F16)[:, 0:D], buffer, ACT.Square,
                                     accum_out=msx[:, i, 0:1]).then_inc(x_sq, 1)

            def x_high(v, buffer, pair_, free):
                act.wait_ge(x_mod, v + 1)
                for wait in free:
                    need(act, *wait)
                nc.scalar.activation(pair_[:, 0], buffer, ACT.Copy).then_inc(x_hi, 1)

            def read_values_low(q):
                count, b = q
                act.wait_ge(pv_done, 4 * count + 4)
                need(act, ov_done, count)
                nc.scalar.activation(o_lo[:], values[:, b, :, DH:2 * DH], ACT.Copy).then_inc(ov_copy, 1)

            def o_high(T, buffer, pair_, waits):
                for wait in waits:
                    need(act, *wait)
                nc.scalar.activation(pair_[:, 0], buffer, ACT.Copy).then_inc(o_hi, 1)

            def read_yT(T, hh, banks):
                act.wait_ge(y_tr, 2 * T + hh + 1)
                act.wait_ge(halo, T + 1)
                nc.scalar.activation(yT[:, hh * HC:(hh + 1) * HC, H:H + P],
                                     banks[hh].rearrange("p (c n) -> p c n", n=P), ACT.Copy).then_inc(y_ev, 1)

            def read_out(T, hh, banks):
                act.wait_ge(f_tr, 2 * T + hh + 1)
                need(act, f_st, 16 * T)
                nc.scalar.activation(fin[:, hh * HW:(hh + 1) * HW], banks[hh], ACT.Copy).then_inc(f_ev, 1)

            def unit(u, par, qkv, xs, outs, fins):
                w, v, T = u + 1, u + LEAD, u - K
                for s in range(NS):
                    if fins and s == 0:
                        read_yT(T - 1, 1, y_banks)
                    if fins and s == at["fin"]:
                        read_out(T - 1, 0, f_banks)
                    for name, hf, i in (("h00", 0, 0), ("h01", 0, 1), ("h02", 0, 2),
                                        ("h10", 1, 0), ("h11", 1, 1), ("h12", 1, 2)):
                        if qkv and s == at[name] + (name != "h01") < NS:
                            read_stacks(w, 1 - par, hf, i)
                    exponent(u, s, par)
                    if s % 4 == 0:
                        q = group(u, s)
                        if q:
                            read_values_low(q)
                    if fins and s == at["fin"]:
                        read_out(T - 1, 1, f_banks)
                    if outs and s == at["ohi"]:
                        o_high(T, o_in[:], pair, ((o_ld, 16 * (T + 1)), (oT_in, 16 * T),
                                                  (xT_in, 16 * (u + 1) if xs else 16 * (U - K))))
                    if qkv and s < K:
                        read_projection(w, s)
                    if xs and s == at["xs"]:
                        x_square(v, par, 2, x_in[:], (x_ld, 16 * (u + 1)), 2 * w)
                    if xs and s == at["xh"]:
                        x_high(v, x_in[:], pair, ((xT_in, 16 * u), (oT_in, 16 * T if fins else 0)))
                    for hf in range(2):
                        if qkv and s == at[f"sq{hf}"]:
                            squares(w, hf)
                        if qkv and s == at[f"hi{hf}"]:
                            high_halves(w, 1 - par, hf)
                    for i in range(3):
                        if qkv and s == at[f"h1{i}"] == NS - 1:
                            read_stacks(w, 1 - par, 1, i)
                    if outs and s == at["yt"]:
                        read_yT(T, 0, y_banks)

            def last_o_high(T, par):
                free = (pT_in[par], 16 * G * U) if isinstance(T, int) and T < U - K + 2 else \
                    (last_oT_in[par], last_loads(T, par) - 16)
                o_high(T, last_o_in[par], last_pair[par], ((last_o_ld[par], last_loads(T, par)), free))

            def last_tile(T, par, first, last):
                if first:
                    read_yT(T - 1, 1, y_banks)
                else:
                    read_yT(T - 1, 1, last_banks["y"])
                if not last:
                    last_o_high(T + 1, 1 - par)
                read_yT(T, 0, last_banks["y"])
                for hh in range(2):
                    read_out(T - 1, hh, last_banks["f"])

            for v in range(LEAD + 2):
                if v >= 2:
                    x_high(v - 2, first_x[(v - 2) % 4], first_pair[(v - 2) % 4],
                           ((first_xT_in[v % 2], 16 * ((v - 6) // 2 + 1)),))
                if v < LEAD:
                    x_square(v, v % 4, 4, first_x[v % 4], (first_x_ld[v % 4], 16 * (v // 4 + 1)), 0)
                if v >= 5 and v - 5 < KH:
                    read_projection(0, v - 5)
            for t in range(LEAD - 3, KH):
                read_projection(0, t)
            squares(0, 0)
            for t in range(KH, K):
                if t == K - 1:
                    high_halves(0, 0, 0)
                read_projection(0, t)
            squares(0, 1)
            for i in range(3):
                read_stacks(0, 0, 0, i)
            high_halves(0, 0, 1)
            for i in range(3):
                read_stacks(0, 0, 1, i)
            in_units(act, unit)
            for i in range(2):
                read_values_low((G * U - 2 + i, i))
            last_o_high(U - K, 0)
            in_last_tiles(act, last_tile)
            read_yT(U - 1, 1, last_banks["y"])
            for hh in range(2):
                read_out(U - 1, hh, last_banks["f"])

        @block.gpsimd
        def _(pool):
            def low(u, s):
                pool.wait_ge(hi_done, slot(u, s) + 1)
                nc.gpsimd.tensor_tensor(p_pair[:, s % 4, 1, :], prob[:, s % 4, :], p_pair[:, s % 4, 0, :],
                                        ALU.subtract).then_inc(lo_done, 1)

            def half_power(w, hf):
                pool.wait_ge(h_ms, 2 * w + hf + 1)
                need(pool, h_n, 2 * (2 * w + hf))
                nc.gpsimd.tensor_tensor(rs[:], ms[:], const["power"][:, 0:4 * KH], ALU.pow).then_inc(h_pw, 1)

            def half_low(w, par, hf):
                n = 2 * w + hf
                pool.wait_ge(h_hi, 3 * n + 3)
                nc.gpsimd.tensor_tensor(q_pair[:, :, DH:2 * DH], stage[:, hf, :, 0:DH], q_pair[:, :, 0:DH],
                                        ALU.subtract).then_inc(h_lo, 1)
                nc.gpsimd.tensor_tensor(k_pair[:, :, DH:2 * DH], stage[:, hf, :, DH:2 * DH], k_pair[:, :, 0:DH],
                                        ALU.subtract).then_inc(h_lo, 1)

            def half_low_values(w, par, hf):
                vp = v_pair[:, par, 2 * KH * hf:2 * KH * (hf + 1), :]
                nc.gpsimd.tensor_tensor(vp[:, :, DH:2 * DH], stage[:, hf, :, 2 * DH:3 * DH], vp[:, :, 0:DH],
                                        ALU.subtract).then_inc(h_lo, 1)

            def x_power(v, i, ring):
                pool.wait_ge(x_ms, v + 1)
                need(pool, x_mul, v - ring + 1)
                nc.gpsimd.tensor_tensor(msx[:, i, 2:3], msx[:, i, 1:2], const["power"][:, 0:1], ALU.pow).then_inc(x_pw, 1)

            def split_low(buffer, pair_, hi, lo, count):
                pool.wait_ge(hi, count)
                nc.gpsimd.tensor_tensor(pair_[:, 1], buffer, pair_[:, 0], ALU.subtract).then_inc(lo, 1)

            def unit(u, par, qkv, xs, outs, fins):
                w, v, T = u + 1, u + LEAD, u - K
                for s in range(NS):
                    if s:
                        low(u, s - 1)
                    elif not (isinstance(u, int) and u == 0):
                        low(u - 1, NS - 1)
                    if xs and s == at["xs"]:
                        x_power(v, par, 2)
                    if xs and s == at["xlo"]:
                        split_low(x_in[:], pair, x_hi, x_lo, v + 1)
                    for hf in range(2):
                        if qkv and s == at[f"ss{hf}"]:
                            half_power(w, hf)
                        if qkv and s == at[f"lo{hf}"]:
                            half_low(w, 1 - par, hf)
                        if qkv and s == at[f"lv{hf}"]:
                            half_low_values(w, 1 - par, hf)
                    if outs and s == at["olo"]:
                        split_low(o_in[:], pair, o_hi, o_low, T + 1)

            for v in range(LEAD + 2):
                if v >= 2:
                    split_low(first_x[(v - 2) % 4], first_pair[(v - 2) % 4], x_hi, x_lo, v - 1)
                if v < LEAD:
                    x_power(v, v % 4, 4)
            for hf in range(2):
                half_power(0, hf)
                half_low(0, 0, hf)
                half_low_values(0, 0, hf)
            in_units(pool, unit)
            low(U - 1, NS - 1)

            def last_tile(T, par, first, last):
                if not last:
                    split_low(last_o_in[1 - par], last_pair[1 - par], o_hi, o_low, T + 2)

            split_low(last_o_in[0], last_pair[0], o_hi, o_low, U - K + 1)
            in_last_tiles(pool, last_tile)

        @block.vector
        def _(dve):
            def maximum(u, s):
                g = slot(u, s)
                dve.wait_ge(qk_done, g + 1)
                nc.vector.tensor_reduce(neg[:, s:s + 1], scores[:, s % 2, 0:N], axis=AX.X, op=ALU.max,
                                        negate=True).then_inc(max_done, 1)
                dve.wait_ge(max_done, g + 1)
                nc.vector.tensor_scalar(bias[:, s:s + 1], neg[:, s:s + 1], const["l_scale"][:, 0:1], P_SHIFT,
                                        ALU.mult, ALU.add).then_inc(bias_done, 1)

            def high(u, s):
                g = slot(u, s)
                dve.wait_ge(exp_done, g + 1)
                need(dve, pT_in[s % 4], 16 * four(u, s))
                nc.vector.tensor_copy(p_pair[:, s % 4, 0, :], prob[:, s % 4, :]).then_inc(hi_done, 1)

            def sums(w, hf):
                n = 2 * w + hf
                dve.wait_ge(h_sq, n + 1)
                nc.vector.tensor_reduce(ms[:], square[:].rearrange("p (t d) -> p t d", d=DH), axis=AX.X,
                                        op=ALU.add).then_inc(h_ss, 1)
                dve.wait_ge(h_ss, n + 1)
                nc.vector.tensor_scalar(ms[:], ms[:], 1.0 / (DH * QK_UP ** 2), const["eps_u"][:, bass.ds(w, 1)],
                                        ALU.mult, ALU.add).then_inc(h_ms, 1)

            def normalise(w, hf):
                n = 2 * w + hf
                dve.wait_ge(h_pw, n + 1)
                qk_ = stage[:, hf, :, 0:2 * DH].rearrange("p t (j d) -> p t j d", d=DH)
                r_ = rs[:].rearrange("p (t j a) -> p t j a", j=2, a=1).to_broadcast([P, 2 * KH, 2, DH])
                nc.vector.tensor_tensor(qk_, qk_, r_, ALU.mult).then_inc(h_n, 1)
                dve.wait_ge(h_n, 2 * n + 1)
                q_ = stage[:, hf, :, 0:DH]
                g_ = const["g_qk"][:].rearrange("p (a d) -> p a d", a=1).to_broadcast([P, 2 * KH, DH])
                nc.vector.tensor_tensor(q_, q_, g_, ALU.mult).then_inc(h_n, 1)

            def x_mean(v, i, ring):
                dve.wait_ge(x_sq, v + 1)
                need(dve, x_pw, v - ring + 1)
                nc.vector.tensor_scalar(msx[:, i, 1:2], msx[:, i, 0:1], 1.0 / D, EPS, ALU.mult, ALU.add).then_inc(x_ms, 1)

            def x_modulate(v, i, buffer):
                dve.wait_ge(x_pw, v + 1)
                dve.wait_ge(rows_in, 16 * (v // K) + 16)
                nc.vector.scalar_tensor_tensor(out=buffer, in0=buffer, scalar=msx[:, i, 2:3], in1=rows[:, 0],
                                               op0=ALU.mult, op1=ALU.mult).then_inc(x_mul, 1)
                dve.wait_ge(x_mul, v + 1)
                nc.vector.tensor_tensor(buffer, buffer, rows[:, 1], ALU.add).then_inc(x_mod, 1)

            def read_values(q, tile, head, col):
                count, b = q
                dve.wait_ge(exp_done, 4 * count + 4)
                nc.vector.reciprocal(inv[:], total[:, col:col + 4]).then_inc(ov_inv, 1)
                dve.wait_ge(ov_copy, count + 1)
                nc.vector.tensor_tensor(o_lo[:], values[:, b, :, 0:DH], o_lo[:], ALU.add).then_inc(ov_add, 1)
                dve.wait_ge(ov_add, count + 1)
                nc.vector.tensor_tensor(
                    o_out[:, tile:tile + 4, head, :], o_lo[:],
                    inv[:].rearrange("p (t a) -> p t a", a=1).to_broadcast([P, 4, DH]), ALU.mult).then_inc(ov_done, 1)

            def values_at(u, s, par):
                q = group(u, s)
                if not q:
                    return
                first = (s - 8) % NS
                upar = par if s >= 8 else 1 - par
                if first == 0:
                    need(dve, o_st, 16 * (u if s >= 8 else u - 1))
                dve_read(q, first, upar)

            def dve_read(q, first, upar):
                need(dve, ov_done, q[0])
                read_values(q, first % K, first // K, upar * NS + first)

            def residual(T, o_, y_, loaded):
                for wait in loaded:
                    dve.wait_ge(*wait)
                nc.vector.scalar_tensor_tensor(out=y_, in0=o_, scalar=const["v_scale"][:, bass.ds(T, 1)],
                                               in1=y_, op0=ALU.mult, op1=ALU.add).then_inc(s_done, 1)

            def add_product(T, n, y_):
                dve.wait_ge(op_mm, 2 * T + n + 1)
                dve.wait_ge(s_done, T + 1)
                ys = y_[:, n * HN:(n + 1) * HN]
                nc.vector.scalar_tensor_tensor(out=ys, in0=misc[:, 1 - n, 0:HN],
                                               scalar=const["y_scale"][:, bass.ds(T, 1)],
                                               in1=ys, op0=ALU.mult, op1=ALU.add).then_inc(op_ev, 1)

            def carry_tokens(T):
                need(dve, cv, TAPS * K * T)
                nc.vector.tensor_scalar(yT[:, :, 0:H], yT[:, :, P:P + H], const["carry"][:, bass.ds(T, 1)], None,
                                        ALU.mult).then_inc(halo, 1)

            def convolve(T, quarter):
                chunks = K // 4
                dve.wait_ge(y_ev, 2 * T + quarter // 2 + 1)
                need(dve, f_tr, 2 * T)
                base = TAPS * K * T + TAPS * chunks * quarter
                for k in range(TAPS - 1, -1, -1):
                    for i in range(chunks):
                        c = quarter * chunks + i
                        if k == TAPS - 1:
                            nc.vector.tensor_scalar(acc[:, c, :], yT[:, c, k:k + P], const["taps"][:, k, c:c + 1],
                                                    const["conv_b"][:, c:c + 1], ALU.mult, ALU.add).then_inc(cv, 1)
                        else:
                            dve.wait_ge(cv, base + chunks * (TAPS - 2 - k) + i + 1)
                            nc.vector.scalar_tensor_tensor(out=acc[:, c, :], in0=yT[:, c, k:k + P],
                                                           scalar=const["taps"][:, k, c:c + 1], in1=acc[:, c, :],
                                                           op0=ALU.mult, op1=ALU.add).then_inc(cv, 1)

            def unit(u, par, qkv, xs, outs, fins):
                w, v, T = u + 1, u + LEAD, u - K
                for s in range(NS):
                    if outs and s == at["a1"] != at["op1b"]:
                        add_product(T, 1, y)
                    maximum(u, s)
                    if outs and s == at["a0"]:
                        add_product(T, 0, y)
                        carry_tokens(T)
                    if s:
                        high(u, s - 1)
                    elif not (isinstance(u, int) and u == 0):
                        high(u - 1, NS - 1)
                    if s % 4 == 0:
                        values_at(u, s, par)
                    if outs and s == at["res"]:
                        residual(T, o_in[:], y[:], ((xo_ld, 16 * (T + 1)), (o_ld, 16 * (T + 1))))
                    if xs and s == at["xs"]:
                        x_mean(v, par, 2)
                    if xs and s == at["xm"]:
                        x_modulate(v, par, x_in[:])
                    for hf in range(2):
                        if qkv and s == at[f"ss{hf}"]:
                            sums(w, hf)
                        if qkv and s == at[f"n{hf}"]:
                            normalise(w, hf)
                    if outs and s == at["a1"] == at["op1b"]:
                        add_product(T, 1, y)
                    for quarter in range(4):
                        if fins and s == at["cv"][quarter]:
                            convolve(T - 1, quarter)

            def last_head(T, par):
                residual(T, last_o_in[par], last_y[par],
                         ((last_x_ld[par], last_loads(T, par)), (last_o_ld[par], last_loads(T, par))))

            def last_tile(T, par, first, last):
                for quarter in range(2):
                    convolve(T - 1, quarter)
                add_product(T, 0, last_y[par])
                for quarter in range(2, 4):
                    convolve(T - 1, quarter)
                carry_tokens(T)
                add_product(T, 1, last_y[par])
                if not last:
                    last_head(T + 1, 1 - par)

            nc.vector.memset(yT[:], 0.0)
            for v in range(LEAD):
                x_mean(v, v % 4, 4)
                x_modulate(v, v % 4, first_x[v % 4])
            for hf in range(2):
                sums(0, hf)
                normalise(0, hf)
            in_units(dve, unit)
            high(U - 1, NS - 1)
            for i in range(2):
                dve_read((G * U - 2 + i, i), NS - 8 + 4 * i, 1)
            last_head(U - K, 0)
            in_last_tiles(dve, last_tile)
            for quarter in range(4):
                convolve(U - 1, quarter)


_INS = ["x", "cond_2048", "L0_cond_W_emb", "L0_cond_b_emb", "L0_cond_g_norm", "L0_cond_W_qkv",
        "L0_cond_g_q", "L0_cond_g_k", "L0_cond_W_out", "L1_cond_b"]


def kernel(**inputs):
    import numpy as _np
    import concourse.bacc as _bacc
    from concourse import mybir as _mybir
    from concourse.bass_utils import run_bass_kernel_spmd as _run

    nc = _bacc.Bacc("TRN2", target_bir_lowering=False, num_devices=1, dynamic_dma_scratch_size=1024)
    arrays, args = {}, []
    for name in _INS:
        a = _np.ascontiguousarray(inputs[name])
        arrays[f"in_{name}"] = a
        args.append(nc.dram_tensor(f"in_{name}", a.shape, _mybir.dt.from_np(a.dtype), kind="ExternalInput").ap())
    args.append(nc.dram_tensor("out_0", inputs["x"].shape, _mybir.dt.float32, kind="ExternalOutput").ap())
    bass_cond_attention_conv(nc, *args)
    r = _run(nc, [arrays], core_ids=[0])
    return r.results[0]["out_0"]
```
